# Optimizing a Trainium2 kernel written in Bass

```python
import numpy as np
import jax
import jax.numpy as jnp

def _softmax(x, axis=-1):
    return jax.nn.softmax(x, axis=axis)

def _gelu(x):
    return jax.nn.gelu(x, approximate=True)

def _silu(x):
    return jax.nn.silu(x)

def _sigmoid(x):
    return jax.nn.sigmoid(x)

def _layernorm(x, axis=-1, eps=1e-05):
    m = jnp.mean(x, axis=axis, keepdims=True)
    v = jnp.var(x, axis=axis, keepdims=True)
    return (x - m) / jnp.sqrt(v + eps)

def _scatter_add(tgt, idx, src, axis=0):
    return tgt.at[idx].add(src)

def _segment_sum(src, seg, n):
    return jax.ops.segment_sum(src, seg, n)
kernel_name = 'mk_prb_d1_jaxref_r8_82943a'

def setup_inputs(seed: int=0):
    np.random.seed(seed)
    _w = jnp.asarray

    def _L0_attn_setup():
        import jax, jax.numpy as jnp
        import numpy as np
        EPS_RMS = 1.1920929e-07

        def rms_norm(x):
            ms = jnp.mean(jnp.square(x), axis=-1, keepdims=True)
            return x * jax.lax.rsqrt(ms + EPS_RMS)

        def parallel_prefix_matmul(M):
            B, T = (M.shape[0], M.shape[1])
            T_pad = 1 << (T - 1).bit_length()
            if T_pad != T:
                eye = jnp.broadcast_to(jnp.eye(2, dtype=M.dtype), (B, T_pad - T, M.shape[2], 2, 2))
                M = jnp.concatenate([M, eye], axis=1)
            S = M
            stride = 1
            while stride < T_pad:
                prod = jnp.matmul(S[:, stride:], S[:, :T_pad - stride])
                S = jnp.concatenate([S[:, :stride], prod], axis=1)
                stride *= 2
            return S[:, :T]
        key = jax.random.key(seed)
        k1, k2, k3, k4 = jax.random.split(key, 4)
        B, T, D, k = (4, 256, 128, 32)
        x = jax.random.normal(k1, (B, T, D), dtype=jnp.float32)
        W_m = jax.random.normal(k2, (k * 4, D), dtype=jnp.float32) / np.sqrt(D)
        v_vec = jax.random.normal(k3, (k, 2, 1), dtype=jnp.float32) * 0.02
        W_proj = jax.random.normal(k4, (D, k * 2), dtype=jnp.float32) / np.sqrt(k * 2)
        out_scale = jnp.ones((D,), dtype=jnp.float32)
        return {'x': x, 'W_m': W_m, 'v_vec': v_vec, 'W_proj': W_proj, 'out_scale': out_scale}
    _L0_attn_in = _L0_attn_setup()

    def _L0_ffn_setup():
        import jax, jax.numpy as jnp
        import numpy as np
        N_EMBD = 128
        N_STATE = 512
        key = jax.random.key(seed)
        k_x, k_w1, k_b1, k_w2, k_b2 = jax.random.split(key, 5)
        x = jax.random.normal(k_x, (4, 256, N_EMBD), dtype=jnp.float32)
        w1 = jax.random.normal(k_w1, (N_EMBD, N_STATE), dtype=jnp.float32) * (1.0 / np.sqrt(N_EMBD))
        b1 = jax.random.normal(k_b1, (N_STATE,), dtype=jnp.float32) * 0.02
        w2 = jax.random.normal(k_w2, (N_STATE, N_EMBD), dtype=jnp.float32) * (1.0 / np.sqrt(N_STATE))
        b2 = jax.random.normal(k_b2, (N_EMBD,), dtype=jnp.float32) * 0.02
        return {'x': x, 'w1': w1, 'b1': b1, 'w2': w2, 'b2': b2}
    _L0_ffn_in = _L0_ffn_setup()
    _d = {'L0_attn_x': _L0_attn_in['x'], 'L0_attn_W_m': _L0_attn_in['W_m'], 'L0_attn_v_vec': _L0_attn_in['v_vec'], 'L0_attn_W_proj': _L0_attn_in['W_proj'], 'L0_attn_out_scale': _L0_attn_in['out_scale'], 'L0_ffn_w1': _L0_ffn_in['w1'], 'L0_ffn_b1': _L0_ffn_in['b1'], 'L0_ffn_w2': _L0_ffn_in['w2'], 'L0_ffn_b2': _L0_ffn_in['b2']}
    _x0 = _d['L0_attn_x']
    _d['L0_attn_x'] = jax.random.normal(jax.random.fold_in(jax.random.key(seed), 1), (16, 256, 128), dtype=_x0.dtype)
    del _x0
    return _d

def reference(L0_attn_x, L0_attn_W_m, L0_attn_v_vec, L0_attn_W_proj, L0_attn_out_scale, L0_ffn_w1, L0_ffn_b1, L0_ffn_w2, L0_ffn_b2):

    def _L0_attn_ref(x, W_m, v_vec, W_proj, out_scale):
        import jax, jax.numpy as jnp
        import numpy as np
        EPS_RMS = 1.1920929e-07

        def rms_norm(x):
            ms = jnp.mean(jnp.square(x), axis=-1, keepdims=True)
            return x * jax.lax.rsqrt(ms + EPS_RMS)

        def parallel_prefix_matmul(M):
            B, T = (M.shape[0], M.shape[1])
            T_pad = 1 << (T - 1).bit_length()
            if T_pad != T:
                eye = jnp.broadcast_to(jnp.eye(2, dtype=M.dtype), (B, T_pad - T, M.shape[2], 2, 2))
                M = jnp.concatenate([M, eye], axis=1)
            S = M
            stride = 1
            while stride < T_pad:
                prod = jnp.matmul(S[:, stride:], S[:, :T_pad - stride])
                S = jnp.concatenate([S[:, :stride], prod], axis=1)
                stride *= 2
            return S[:, :T]
        B, T, D = x.shape
        k = v_vec.shape[0]
        residual = x
        xn = rms_norm(x)
        M = (xn @ W_m.T).reshape(B, T, k, 2, 2)
        norms = jnp.sqrt(jnp.sum(jnp.square(M), axis=(-2, -1), keepdims=True))
        M = M / jnp.maximum(norms, 1e-06)
        S = parallel_prefix_matmul(M)
        h = jnp.matmul(S, v_vec[None, None]).squeeze(-1)
        h = h.reshape(B, T, k * 2)
        out = h @ W_proj.T
        return residual + out_scale[None, None, :] * out

    def _L0_ffn_ref(x, w1, b1, w2, b2):
        import jax, jax.numpy as jnp
        import numpy as np
        N_EMBD = 128
        N_STATE = 512
        h = jax.nn.gelu(jnp.einsum('bse,eh->bsh', x, w1) + b1, approximate=False)
        return jnp.einsum('bsh,he->bse', h, w2) + b2
    x = L0_attn_x
    xn = _layernorm(x, axis=-1)
    x = x + _L0_attn_ref(xn, L0_attn_W_m, L0_attn_v_vec, L0_attn_W_proj, L0_attn_out_scale) + _L0_ffn_ref(xn, L0_ffn_w1, L0_ffn_b1, L0_ffn_w2, L0_ffn_b2)
    return x

_drawn_inputs = setup_inputs


def setup_inputs(seed=0):
    import zlib

    import numpy as np

    out = dict(_drawn_inputs(seed))
    spreads = {'L0_attn_out_scale': (1.0, 0.6)}
    factors = {'L0_attn_W_m': 8.0,
     'L0_attn_v_vec': 8.0,
     'L0_attn_W_proj': 8.0,
     'L0_ffn_b1': 8.0,
     'L0_ffn_b2': 5.83}
    for name, (base, spread) in spreads.items():
        noise = np.random.default_rng([zlib.crc32(name.encode()), seed]).standard_normal(out[name].shape)
        drawn = base * np.exp(spread * noise) if base else spread * noise
        out[name] = jnp.asarray(drawn.astype(out[name].dtype))
    for name, factor in factors.items():
        out[name] = (out[name] * factor).astype(out[name].dtype)
    return out
```

```python
from contextlib import ExitStack

import concourse.bass as bass
from concourse import mybir

F32 = mybir.dt.float32
F32R = mybir.dt.float32r
ALU = mybir.AluOpType
ACT = mybir.ActivationFunctionType

LN_EPS = 1e-5
RMS_EPS = 1.1920929e-07
NORM_FLOOR = 1e-6


def block_kernel(nc, x, W_m, v_vec, W_proj, out_scale, w1, b1, w2, b2, out):
    B, T, D = x.shape
    K = v_vec.shape[0]
    NH = w1.shape[1]
    P = 128
    G = P // K
    NB = B // G
    NT = T // P
    NJ = NB * NT
    HC = NH // P
    IJ = 4
    CH = G * P
    NP = NJ // 2
    L = 16
    C = T // L
    BH = NB // 2
    S = BH * C
    CT = P // L
    assert (P, G, NJ, D) == (128, 4, 8, 128) and K * G == P and C == 16

    x_v = x.rearrange("(g b) (h p) d -> b h p g d", g=G, p=P)
    out_v = out.rearrange("(g b) (h p) d -> b h p g d", g=G, p=P)

    ctx = ExitStack()
    with ctx:
        def sb(name, shape, dt=F32):
            return ctx.enter_context(nc.sbuf_tensor(name, shape, dt))

        def sem(name):
            return ctx.enter_context(nc.semaphore(name))

        ident = sb("ident", [P, P])
        wmT = sb("wmT", [P, IJ * K])
        w1_sb = sb("w1_sb", [P, NH])
        w1_hi = sb("w1_hi", [P, NH], F32R)
        w1_lo = sb("w1_lo", [P, NH], F32R)
        w2_sb = sb("w2_sb", [P, HC, D])
        b1_sb = sb("b1_sb", [P, HC])
        b2_sb = sb("b2_sb", [P, D])
        wp_rep = sb("wp_rep", [P, 2, D])
        osc_sb = sb("osc_sb", [P, D])
        wp_bd = sb("wp_bd", [P, 2, G * D])
        v_sb = sb("v_sb", [P, 2])

        x_sb = sb("x_sb", [P, NJ, G, D])
        xn = sb("xn", [P, NJ, G, D])
        stats = sb("stats", [P, NJ, G, 6])
        mv = sb("mv", [P, NJ, G, 2])
        sd = sb("sd", [P, NJ, G])
        rstd = sb("rstd", [P, NJ, G])
        nmr = sb("nmr", [P, NJ, G])
        ms_a = sb("ms_a", [P, NJ, G])
        ms_b = sb("ms_b", [P, NJ, G])
        floor = sb("floor", [P, NJ, G])
        xT = sb("xT", [P, 4, CH])
        xT_hi = sb("xT_hi", [P, 4, CH], F32R)
        xT_lo = sb("xT_lo", [P, 4, CH], F32R)
        sq = sb("sq", [P, 2, G, IJ, K])
        sq2 = sb("sq2", [P, 2 * G, 2, K])
        nsq0 = sb("nsq0", [P, 2 * G, K])
        nsq = sb("nsq", [P, 2 * G, K])
        nrm = sb("nrm", [P, 2, G, K])
        winv = sb("winv", [P, 2, G, K])
        Mn = sb("Mn", [P, 2, IJ, G, K])
        MT = sb("MT", [P, 2, L, IJ, S])
        ST = sb("ST", [P, 2, L, 2, 2, S])
        PR = sb("PR", [P, 2, 2, 2, 2, S])
        UP = sb("UP", [P, 2, 2, 2, S // 2])
        UU = sb("UU", [P, 2, 2, S // 2])
        WP = sb("WP", [P, 2, 2, 2, S // 4])
        WW = sb("WW", [P, 2, 2, S // 4])
        HP = sb("HP", [P, 2, 2, S // 2])
        HS = sb("HS", [P, 2, 2, S])
        AP_ = sb("AP_", [P, 2, L, 2, S])
        h = sb("h", [P, 2, 2, BH, T])
        g_sb = sb("g_sb", [P, HC, NJ, CH])

        ps = [ctx.enter_context(nc.psum_tensor(f"bank{i}", [P, CH], F32)) for i in range(8)]
        T_BANK, M_BANK, F_BANK, O_BANK = (0, 1), (2, 3), (4, 5), (6, 7, 0, 1, 2, 3, 4, 5)

        x_loaded = [sem(f"x_loaded{j}") for j in range(NJ)]
        wm_loaded, w1_loaded, w2_loaded = sem("wm_loaded"), sem("w1_loaded"), sem("w2_loaded")
        b_loaded, wp_loaded, v_loaded = sem("b_loaded"), sem("wp_loaded"), sem("v_loaded")
        out_stored = sem("out_stored")
        zeroed, ident_ready = sem("zeroed"), sem("ident_ready")
        bn_done, mv_ready, sd_ready = sem("bn_done"), sem("mv_ready"), sem("sd_ready")
        rstd_ready, nmr_ready, xn_ready = sem("rstd_ready"), sem("nmr_ready"), sem("xn_ready")
        ms_step, floor_ready, resid_ready = sem("ms_step"), sem("floor_ready"), sem("resid_ready")
        resid_half = sem("resid_half")
        xT_done, xT_ready, hi_ready, lo_ready = sem("xT_done"), sem("xT_ready"), sem("hi_ready"), sem("lo_ready")
        m_done, sq_ready = sem("m_done"), sem("sq_ready")
        nsq_step, nsq_ready, nrm_ready = sem("nsq_step"), sem("nsq_ready"), sem("nrm_ready")
        winv_ready, mn_ready = sem("winv_ready"), sem("mn_ready")
        mt_done, mt_ready = sem("mt_done"), sem("mt_ready")
        prod_ready, state_ready = sem("prod_ready"), sem("state_ready")
        seg_step, h_ready = sem("seg_step"), sem("h_ready")
        f1_done, gelu_ready = sem("f1_done"), sem("gelu_ready")
        y_done, y_ready = sem("y_done"), sem("y_ready")
        w1hi_ready, w1_ready = sem("w1hi_ready"), sem("w1_ready")
        bd_zeroed, bd_ready = sem("bd_zeroed"), sem("bd_ready")
        hs_ready = sem("hs_ready")

        block = ctx.enter_context(nc.Block())

        @block.sync
        def _(sp):
            for j in range(NJ):
                sp.dma_start(x_sb[:, j], x_v[j // NT, j % NT]).then_inc(x_loaded[j], 16)
                if j == 1:
                    sp.dma_start(wmT[:, :], W_m).then_inc(wm_loaded, 16)
                    sp.dma_start(w1_sb[:, :], w1).then_inc(w1_loaded, 16)
                if j == 3:
                    sp.dma_start(b1_sb[:, :], b1).then_inc(b_loaded, 16)
            sp.dma_start(b2_sb[:, :], b2.rearrange("(a d) -> a d", a=1).broadcast_to([P, D])).then_inc(b_loaded, 16)
            sp.dma_start(w2_sb[:, :, :], w2.rearrange("(c p) e -> p c e", p=P)).then_inc(w2_loaded, 16)
            sp.dma_start(osc_sb[:, :], out_scale.rearrange("(a d) -> a d", a=1).broadcast_to([P, D])
                         ).then_inc(wp_loaded, 16)
            for g in range(G):
                sp.dma_start(wp_rep[g * K:(g + 1) * K, :, :], W_proj).then_inc(wp_loaded, 16)
                sp.dma_start(v_sb[g * K:(g + 1) * K, :], v_vec.rearrange("k i a -> k (i a)")).then_inc(v_loaded, 16)
            for j in range(NJ):
                sp.wait_ge(y_ready, j + 1)
                sp.dma_start(out_v[j // NT, j % NT], x_sb[:, j]).then_inc(out_stored, 16)
            sp.wait_ge(out_stored, 16 * NJ)

        @block.gpsimd
        def _(pool):
            nc.gpsimd.memset(ident[:, :], 0.0).then_inc(zeroed, 1)
            pool.wait_ge(zeroed, 1)
            nc.gpsimd.affine_select(out=ident[:, :], in_=ident[:, :], compare_op=ALU.not_equal, fill=1.0, base=0,
                                    pattern=[[-1, P]], channel_multiplier=1).then_inc(ident_ready, 1)
            nc.gpsimd.memset(wp_bd[:, :, :], 0.0).then_inc(bd_zeroed, 1)
            for p in range(NP):
                js = slice(2 * p, 2 * p + 2)
                pool.wait_ge(rstd_ready, p + 1)
                nc.gpsimd.tensor_tensor(ms_a[:, js], mv[:, js, :, 1], rstd[:, js], ALU.mult).then_inc(ms_step, 1)
                pool.wait_ge(ms_step, 2 * p + 1)
                nc.gpsimd.tensor_tensor(ms_b[:, js], ms_a[:, js], rstd[:, js], ALU.mult).then_inc(ms_step, 1)
                pool.wait_ge(ms_step, 2 * p + 2)
                nc.gpsimd.tensor_scalar(floor[:, js], ms_b[:, js], NORM_FLOOR * NORM_FLOOR,
                                        RMS_EPS * NORM_FLOOR * NORM_FLOOR, ALU.mult, ALU.add).then_inc(floor_ready, 1)
                for j in (2 * p, 2 * p + 1):
                    pool.wait_ge(xn_ready, j + 1)
                    nc.gpsimd.tensor_tensor(x_sb[:, j], x_sb[:, j], xn[:, j], ALU.add).then_inc(resid_half, 1)
            pool.wait_ge(bd_zeroed, 1)
            pool.wait_ge(wp_loaded, 16 * (1 + G))
            for g in range(G):
                rows = slice(g * K, (g + 1) * K)
                if g == 0:
                    pool.wait_ge(resid_half, NJ)
                else:
                    pool.wait_ge(bd_ready, g)
                nc.gpsimd.tensor_tensor(wp_bd[rows, :, g * D:(g + 1) * D], wp_rep[rows, :, :],
                                        osc_sb[rows, :].unsqueeze(1).broadcast_to([K, 2, D]),
                                        ALU.mult).then_inc(bd_ready, 1)
            pool.wait_ge(bd_ready, G)
            pool.wait_ge(b_loaded, 32)
            for j in range(NJ):
                pool.wait_ge(resid_half, j + 1)
                nc.gpsimd.tensor_tensor(x_sb[:, j], x_sb[:, j], b2_sb[:, :].unsqueeze(1).broadcast_to([P, G, D]),
                                        ALU.add).then_inc(resid_ready, 1)

        @block.scalar
        def _(act):
            def std_dev(p):
                act.wait_ge(mv_ready, p + 1)
                js = slice(2 * p, 2 * p + 2)
                nc.scalar.activation(sd[:, js], mv[:, js, :, 1], ACT.Sqrt, bias=LN_EPS).then_inc(sd_ready, 1)

            def take_xT(j):
                act.wait_ge(xT_done, j + 1)
                if j >= 4:
                    act.wait_ge(m_done, j - 3)
                nc.scalar.copy(xT[:, j % 4], ps[T_BANK[j % 2]][:, :]).then_inc(xT_ready, 1)
                if j >= 4:
                    act.wait_ge(f1_done, HC * (j - 3))
                nc.scalar.copy(xT_hi[:, j % 4], ps[T_BANK[j % 2]][:, :]).then_inc(hi_ready, 1)

            def squares(j):
                act.wait_ge(m_done, j + 1)
                if j >= 2:
                    act.wait_ge(nsq_step, 2 * (j // 2) - 1)
                nc.scalar.activation(sq[:, j % 2], ps[M_BANK[j % 2]][:, :], ACT.Square).then_inc(sq_ready, 1)

            def norms(p):
                act.wait_ge(nsq_ready, p + 1)
                if p >= 1:
                    act.wait_ge(winv_ready, p)
                nc.scalar.activation(nrm[:, :, :, :], nsq[:, :, :], ACT.Sqrt).then_inc(nrm_ready, 1)

            def take_MT(j):
                half, jj = j // 4, j % 4
                lane = (jj // NT) * C + (jj % NT) * CT
                act.wait_ge(mt_done, j + 1)
                src = ps[M_BANK[j % 2]][:, :].rearrange("p (a c l) -> p a l c", a=IJ, l=L)
                dst = MT[:, half, :, :, lane:lane + CT].rearrange("p l a c -> p a l c")
                nc.scalar.copy(dst, src).then_inc(mt_ready, 1)

            def gelus(j):
                for c in range(HC):
                    act.wait_ge(f1_done, HC * j + c + 1)
                    nc.scalar.activation(g_sb[:, c, j], ps[F_BANK[c % 2]][:, :], ACT.Gelu,
                                         bias=b1_sb[:, c:c + 1]).then_inc(gelu_ready, 1)

            std_dev(0)
            take_xT(0)
            take_xT(1)
            squares(0)
            squares(1)
            for p in range(NP):
                if p + 1 < NP:
                    std_dev(p + 1)
                norms(p)
                if p == 0:
                    act.wait_ge(b_loaded, 32)
                gelus(2 * p)
                take_MT(2 * p)
                take_MT(2 * p + 1)
                if p + 1 < NP:
                    take_xT(2 * p + 2)
                    take_xT(2 * p + 3)
                gelus(2 * p + 1)
                if p + 1 < NP:
                    squares(2 * p + 2)
                    squares(2 * p + 3)

        @block.tensor
        def _(pe):
            def transpose_x(j):
                pe.wait_ge(xn_ready, j + 1)
                if j >= 2:
                    pe.wait_ge(hi_ready, j - 1)
                    pe.wait_ge(lo_ready, j - 1)
                for g in range(G):
                    mm = nc.tensor.transpose(ps[T_BANK[j % 2]][:, g * P:(g + 1) * P], xn[:, j, g, :], ident[:, :])
                mm.then_inc(xT_done, 1)

            def matrices(j):
                pe.wait_ge(xT_ready, j + 1)
                if j == 0:
                    pe.wait_ge(wm_loaded, 16)
                if j >= 2:
                    pe.wait_ge(mt_ready, j - 1)
                for g in range(G):
                    mm = nc.tensor.matmul(ps[M_BANK[j % 2]][:, g * P:(g + 1) * P], xT[:, j % 4, g * P:(g + 1) * P],
                                          wmT[:, :], start=True, stop=True)
                mm.then_inc(m_done, 1)

            def transpose_M(j):
                pe.wait_ge(mn_ready, j + 1)
                for a in range(IJ):
                    mm = nc.tensor.transpose(ps[M_BANK[j % 2]][:, a * P:(a + 1) * P], Mn[:, j % 2, a], ident[:, :])
                mm.then_inc(mt_done, 1)

            def ffn_in(j):
                if j == 0:
                    pe.wait_ge(w1_ready, 1)
                pe.wait_ge(hi_ready, j + 1)
                for c in range(HC):
                    if HC * j + c >= 2:
                        pe.wait_ge(gelu_ready, HC * j + c - 1)
                    bank, cols = ps[F_BANK[c % 2]], slice(c * P, (c + 1) * P)
                    nc.tensor.matmul(bank[:, :], w1_hi[:, cols], xT_hi[:, j % 4], start=True, stop=False)
                    nc.tensor.matmul(bank[:, :], w1_lo[:, cols], xT_hi[:, j % 4], start=False, stop=False)
                    if c == 0:
                        pe.wait_ge(lo_ready, j + 1)
                    nc.tensor.matmul(bank[:, :], w1_hi[:, cols], xT_lo[:, j % 4], start=False,
                                     stop=True).then_inc(f1_done, 1)

            def ffn_out(j):
                bank = ps[O_BANK[j]]
                if j == 0:
                    pe.wait_ge(w2_loaded, 16)
                pe.wait_ge(gelu_ready, HC * (j + 1) if j < 6 else HC * NJ)
                if j in (2, 3):
                    pe.wait_ge(lo_ready, NJ)
                    pe.wait_ge(hi_ready, NJ)
                if j in (4, 5):
                    pe.wait_ge(mt_ready, NJ)
                for g in range(G):
                    for c in range(HC):
                        nc.tensor.matmul(bank[:, g * D:(g + 1) * D], g_sb[:, c, j, g * P:(g + 1) * P], w2_sb[:, c],
                                         start=(g == 0 and c == 0), stop=False, skip_group_check=True)

            def project(j):
                half, jj = j // 4, j % 4
                pe.wait_ge(h_ready, half + 1)
                if j == 0:
                    pe.wait_ge(bd_ready, G)
                bank, tok = ps[O_BANK[j]], slice((jj % NT) * P, (jj % NT + 1) * P)
                for i in range(2):
                    mm = nc.tensor.matmul(bank[:, :], h[:, half, i, jj // NT, tok], wp_bd[:, i],
                                          start=False, stop=(i == 1), skip_group_check=True)
                mm.then_inc(y_done, 1)

            pe.wait_ge(ident_ready, 1)
            transpose_x(0)
            transpose_x(1)
            matrices(0)
            matrices(1)
            for p in range(NP):
                ffn_in(2 * p)
                transpose_M(2 * p)
                transpose_M(2 * p + 1)
                if p + 1 < NP:
                    transpose_x(2 * p + 2)
                    transpose_x(2 * p + 3)
                ffn_in(2 * p + 1)
                if p + 1 < NP:
                    matrices(2 * p + 2)
                    matrices(2 * p + 3)
                if p == 2:
                    ffn_out(0)
            for j in range(1, 4):
                ffn_out(j)
            for j in range(4):
                project(j)
            for j in range(4, NJ):
                ffn_out(j)
            for j in range(4, NJ):
                project(j)

        @block.vector
        def _(dve):
            steps = {"seg": 0, "prod": 0, "state": 0}

            def moments(p):
                for j in (2 * p, 2 * p + 1):
                    dve.wait_ge(x_loaded[j], 16)
                    for g in range(G):
                        nc.vector.bn_stats(stats[:, j, g], x_sb[:, j, g]).then_inc(bn_done, 1)
                for j in (2 * p, 2 * p + 1):
                    for g in range(G):
                        dve.wait_ge(bn_done, G * j + g + 1)
                        last = nc.vector.bn_aggr(mv[:, j, g], stats[:, j, g])
                last.then_inc(mv_ready, 1)

            def layernorm(p):
                js = slice(2 * p, 2 * p + 2)
                dve.wait_ge(sd_ready, p + 1)
                nc.vector.reciprocal(rstd[:, js], sd[:, js]).then_inc(rstd_ready, 1)
                dve.wait_ge(rstd_ready, p + 1)
                nc.vector.scalar_tensor_tensor(nmr[:, js], mv[:, js, :, 0], -1.0, rstd[:, js],
                                               ALU.mult, ALU.mult).then_inc(nmr_ready, 1)
                dve.wait_ge(nmr_ready, p + 1)
                for j in (2 * p, 2 * p + 1):
                    for g in range(G):
                        last = nc.vector.tensor_scalar(xn[:, j, g], x_sb[:, j, g], rstd[:, j, g:g + 1],
                                                       nmr[:, j, g:g + 1], ALU.mult, ALU.add)
                    last.then_inc(xn_ready, 1)

            def low_part(j):
                dve.wait_ge(hi_ready, j + 1)
                if j >= 4:
                    dve.wait_ge(f1_done, HC * (j - 3))
                nc.vector.tensor_tensor(xT_lo[:, j % 4], ps[T_BANK[j % 2]][:, :],
                                        xT_hi[:, j % 4].bitcast(F32), ALU.subtract).then_inc(lo_ready, 1)

            def squared_norms(p):
                s4 = sq[:, :, :, :, :].rearrange("p j g a k -> p (j g) a k")
                dve.wait_ge(sq_ready, 2 * p + 2)
                nc.vector.tensor_tensor(sq2[:, :, :, :], s4[:, :, 0:2], s4[:, :, 2:4], ALU.add).then_inc(nsq_step, 1)
                dve.wait_ge(nsq_step, 2 * p + 1)
                nc.vector.tensor_tensor(nsq0[:, :, :], sq2[:, :, 0], sq2[:, :, 1], ALU.add).then_inc(nsq_step, 1)
                dve.wait_ge(nsq_step, 2 * p + 2)
                dve.wait_ge(floor_ready, p + 1)
                if p >= 1:
                    dve.wait_ge(nrm_ready, p)
                fl = floor[:, 2 * p:2 * p + 2].rearrange("p j g -> p (j g)").unsqueeze(2).broadcast_to([P, 2 * G, K])
                nc.vector.tensor_tensor(nsq[:, :, :], nsq0[:, :, :], fl, ALU.max).then_inc(nsq_ready, 1)

            def normalise(p):
                dve.wait_ge(nrm_ready, p + 1)
                nc.vector.reciprocal(winv[:, :, :, :], nrm[:, :, :, :]).then_inc(winv_ready, 1)
                dve.wait_ge(winv_ready, p + 1)
                for j in (2 * p, 2 * p + 1):
                    if j >= 2:
                        dve.wait_ge(mt_done, j - 1)
                    src = ps[M_BANK[j % 2]][:, :].rearrange("p (g a k) -> p a g k", g=G, a=IJ)
                    w = winv[:, j % 2].unsqueeze(1).broadcast_to([P, IJ, G, K])
                    nc.vector.tensor_tensor(Mn[:, j % 2], src, w, ALU.mult).then_inc(mn_ready, 1)

            def multiply(out4, a, b, lanes):
                return nc.vector.tensor_tensor(out4, a.unsqueeze(2).broadcast_to([P, 2, 2, 2 * lanes]),
                                               b.unsqueeze(1).broadcast_to([P, 2, 2, 2 * lanes]), ALU.mult)

            def scan_step(half, l):
                if l == 0:
                    dve.wait_ge(mt_ready, 4 * (half + 1))
                    steps["state"] += 1
                    nc.vector.tensor_copy(ST[:, half, 0], MT[:, half, 0].rearrange("p (i c) s -> p c i s", i=2)
                                          ).then_inc(state_ready, 1)
                    return
                pr = PR[:, l % 2]
                dve.wait_ge(state_ready, steps["state"])
                multiply(pr.rearrange("p i c k s -> p i c (k s)"),
                         MT[:, half, l].rearrange("p (i k) s -> p i (k s)", i=2),
                         ST[:, half, l - 1].rearrange("p c k s -> p c (k s)"), S).then_inc(prod_ready, 1)
                steps["prod"] += 1
                dve.wait_ge(prod_ready, steps["prod"])
                nc.vector.tensor_tensor(ST[:, half, l].rearrange("p c i s -> p i c s"), pr[:, :, :, 0],
                                        pr[:, :, :, 1], ALU.add).then_inc(state_ready, 1)
                steps["state"] += 1

            def seg(ins):
                ins.then_inc(seg_step, 1)
                steps["seg"] += 1
                return steps["seg"]

            def compose(dst, tmp, later, earlier, n):
                for k in range(2):
                    done = seg(nc.vector.tensor_tensor(
                        tmp[:, k], later[:, k].unsqueeze(1).broadcast_to([P, 2, 2, n]),
                        earlier[:, :, k].unsqueeze(2).broadcast_to([P, 2, 2, n]), ALU.mult))
                dve.wait_ge(seg_step, done)
                done = seg(nc.vector.tensor_tensor(dst, tmp[:, 0], tmp[:, 1], ALU.add))
                dve.wait_ge(seg_step, done)

            def carry(dst, mat, vec, n):
                tmp = HP[:, :, :, 0:n]
                done = seg(nc.vector.tensor_tensor(tmp, mat, vec.unsqueeze(2).broadcast_to([P, 2, 2, n]), ALU.mult))
                dve.wait_ge(seg_step, done)
                done = seg(nc.vector.tensor_tensor(dst, tmp[:, 0], tmp[:, 1], ALU.add))
                dve.wait_ge(seg_step, done)

            def segment_starts(half):
                tot = ST[:, half, L - 1]
                hs = HS[:, half]
                dve.wait_ge(state_ready, steps["state"])
                compose(UU[:, :, :, :], UP, tot[:, :, :, 1::2], tot[:, :, :, 0::2], S // 2)
                compose(WW[:, :, :, :], WP, UU[:, :, :, 1::2], UU[:, :, :, 0::2], S // 4)
                for q in range(3):
                    carry(hs[:, :, 4 * q + 4::C], WW[:, :, :, q::C // 4], hs[:, :, 4 * q::C], BH)
                carry(hs[:, :, 2::4], UU[:, :, :, 0::2], hs[:, :, 0::4], S // 4)
                carry(hs[:, :, 1::2], tot[:, :, :, 0::2], hs[:, :, 0::2], S // 2)

            def apply_starts(half):
                hs = HS[:, half]
                for c in range(2):
                    done = seg(nc.vector.tensor_tensor(
                        AP_[:, c], ST[:, half, :, c],
                        hs[:, c].unsqueeze(1).unsqueeze(1).broadcast_to([P, L, 2, S]), ALU.mult))
                dve.wait_ge(seg_step, done)
                dst = h[:, half].rearrange("p i b (c l) -> p l i (b c)", l=L)
                nc.vector.tensor_tensor(dst, AP_[:, 0], AP_[:, 1], ALU.add).then_inc(h_ready, 1)

            def output(j):
                dve.wait_ge(y_done, j + 1)
                dve.wait_ge(resid_ready, j + 1)
                nc.vector.tensor_tensor(x_sb[:, j].rearrange("p g d -> p (g d)"), ps[O_BANK[j]][:, :],
                                        x_sb[:, j].rearrange("p g d -> p (g d)"), ALU.add).then_inc(y_ready, 1)

            moments(0)
            layernorm(0)
            dve.wait_ge(w1_loaded, 16)
            nc.vector.tensor_copy(w1_hi[:, :], w1_sb[:, :]).then_inc(w1hi_ready, 1)
            moments(1)
            dve.wait_ge(w1hi_ready, 1)
            nc.vector.tensor_tensor(w1_lo[:, :], w1_sb[:, :], w1_hi[:, :].bitcast(F32),
                                    ALU.subtract).then_inc(w1_ready, 1)
            low_part(0)
            low_part(1)
            for p in range(NP):
                squared_norms(p)
                if p + 1 < NP:
                    layernorm(p + 1)
                normalise(p)
                if p == 0:
                    dve.wait_ge(v_loaded, 16 * G)
                    for half in range(2):
                        last = nc.vector.tensor_copy(HS[:, half, :, 0::C],
                                                     v_sb[:, :].unsqueeze(2).broadcast_to([P, 2, BH]))
                    last.then_inc(hs_ready, 1)
                    dve.wait_ge(hs_ready, 1)
                if p + 2 < NP:
                    moments(p + 2)
                if p == 2:
                    for l in range(0, 8):
                        scan_step(0, l)
                if p + 1 < NP:
                    low_part(2 * p + 2)
                    low_part(2 * p + 3)
            for l in range(8, L):
                scan_step(0, l)
            segment_starts(0)
            apply_starts(0)
            for l in range(L):
                scan_step(1, l)
                if l in (6, 9, 12, 15):
                    output((l - 6) // 3)
            segment_starts(1)
            apply_starts(1)
            for j in range(4, NJ):
                output(j)


_INS = ['L0_attn_x', 'L0_attn_W_m', 'L0_attn_v_vec', 'L0_attn_W_proj', 'L0_attn_out_scale',
        'L0_ffn_w1', 'L0_ffn_b1', 'L0_ffn_w2', 'L0_ffn_b2']
_OUTS = [((16, 256, 128), 'float32')]


def kernel(**inputs):
    import numpy as _np
    import concourse.bacc as _bacc
    from concourse import mybir as _mybir
    from concourse.bass_utils import run_bass_kernel_spmd as _run

    nc = _bacc.Bacc("TRN2", target_bir_lowering=False, num_devices=1)
    laid = dict(inputs)
    laid['L0_attn_W_m'] = _np.asarray(inputs['L0_attn_W_m']).reshape(32, 4, 128).transpose(2, 1, 0).reshape(128, 128)
    laid['L0_attn_W_proj'] = _np.asarray(inputs['L0_attn_W_proj']).reshape(128, 32, 2).transpose(1, 2, 0)
    laid['L0_ffn_b1'] = _np.asarray(inputs['L0_ffn_b1']).reshape(4, 128).T
    arrays, args = {}, []
    for name in _INS:
        a = _np.ascontiguousarray(laid[name])
        arrays[f"in_{name}_dram"] = a
        args.append(nc.dram_tensor(f"in_{name}_dram", a.shape, _mybir.dt.from_np(a.dtype), kind="ExternalInput").ap())
    for i, (shape, dtype) in enumerate(_OUTS):
        dt = _mybir.dt.from_np(_np.dtype(dtype))
        args.append(nc.dram_tensor(f"out_{i}_dram", shape, dt, kind="ExternalOutput").ap())
    block_kernel(nc, *args)
    r = _run(nc, [arrays], core_ids=[0])
    got = tuple(r.results[0][f"out_{i}_dram"] for i in range(len(_OUTS)))
    return got[0]
```

```python
import itertools
from contextlib import ExitStack

import concourse.bass as bass
from concourse import mybir

F32 = mybir.dt.float32
F32R = mybir.dt.float32r
ALU = mybir.AluOpType
ACT = mybir.ActivationFunctionType

LN_EPS = 1e-5
RMS_EPS = 1.1920929e-07
NORM_FLOOR = 1e-6

RSQRT_MAGIC = float(0x5F1FFFF9)
RSQRT_A, RSQRT_B = 0.703952253, 0.703952253 * 2.38924456
RSQRT_C = 1.5 + 3e-7

WARM_UP = 12


def block_kernel(nc, x, W_m, v_vec, W_proj, out_scale, w1, b1, w2, b2, out):
    B, T, D = x.shape
    K = v_vec.shape[0]
    NH = w1.shape[1]
    P = 128
    G = P // K
    NB = B // G
    NT = T // P
    NJ = NB * NT
    HC = NH // P
    IJ = 4
    CH = G * P
    L = 8
    S = T // L
    CT = P // L
    assert (P, G, NJ, D, NT) == (128, 4, 8, 128, 2) and K * G == P and S == 32

    x_v = x.rearrange("(g b) (h p) d -> b h p g d", g=G, p=P)
    out_v = out.rearrange("(g b) (h p) d -> b h p g d", g=G, p=P)

    ctx = ExitStack()
    with ctx:
        def sb(name, shape, dt=F32):
            return ctx.enter_context(nc.sbuf_tensor(name, shape, dt))

        def sem(name):
            return ctx.enter_context(nc.semaphore(name))

        ident = sb("ident", [P, P])
        wmT = sb("wmT", [P, IJ * K])
        w1_sb = sb("w1_sb", [P, NH])
        w1_hi = sb("w1_hi", [P, NH], F32R)
        w1_lo = sb("w1_lo", [P, NH], F32R)
        w2_sb = sb("w2_sb", [P, HC, D])
        b1_sb = sb("b1_sb", [P, HC])
        b2_sb = sb("b2_sb", [P, D])
        wp_rep = sb("wp_rep", [P, D])
        osc_sb = sb("osc_sb", [P, D])
        wp_bd = sb("wp_bd", [P, 2, D])
        v_sb = sb("v_sb", [P, 2])

        x_sb = sb("x_sb", [P, NJ, G, D])
        xn = sb("xn", [P, NJ, G, D])
        stats = sb("stats", [P, NJ, G, 6])
        mv = sb("mv", [P, NJ, G, 2])
        sd = sb("sd", [P, NJ, G])
        rstd = sb("rstd", [P, NJ, G])
        nmr = sb("nmr", [P, NJ, G])
        ms_a = sb("ms_a", [P, NJ, G])
        ms_b = sb("ms_b", [P, NJ, G])
        floor = sb("floor", [P, NJ, G])
        xT = sb("xT", [P, 4, CH])
        xT_hi = sb("xT_hi", [P, 4, CH], F32R)
        xT_lo = sb("xT_lo", [P, 4, CH], F32R)
        sq = sb("sq", [P, 2, G, IJ, K])
        sq2 = sb("sq2", [P, 2 * G, 2, K])
        nsq0 = sb("nsq0", [P, 2 * G, K])
        nsq = sb("nsq", [P, 2 * G, K])
        vv = sb("vv", [P, 2, 4 * G])
        lv = sb("lv", [P, 4, 4 * G])
        ry = sb("ry", [P, 2 * G, K])
        ry1 = sb("ry1", [P, 2 * G, K])
        ra = sb("ra", [P, 2 * G, K])
        rb = sb("rb", [P, 2 * G, K])
        winv = sb("winv", [P, 2, G, K])
        Mn = sb("Mn", [P, 2, IJ, G, K])
        MT = sb("MT", [P, NB, L, IJ, S])
        ST = sb("ST", [P, NB, L, 2, 2, S])
        PR = sb("PR", [P, 2, 2, 2, 2, S])
        CP = sb("CP", [P, 2, 2, 2, 2, S // 2])
        SEG2 = sb("SEG2", [P, 2, 2, 2, S // 2])
        SEG4 = sb("SEG4", [P, 2, 2, 2, S // 4])
        SEG8 = sb("SEG8", [P, 2, 2, 2, S // 8])
        HP = sb("HP", [P, 2, 2, 2, S // 2])
        HS = sb("HS", [P, NB, 2, S])
        h = sb("h", [P, NB, 2, T])
        hr = sb("hr", [P, NB, 2, T])
        g_sb = sb("g_sb", [P, HC, NJ, CH])

        ps = [ctx.enter_context(nc.psum_tensor(f"bank{i}", [P, CH], F32)) for i in range(8)]
        T_BANK, M_BANK, F_BANK, O_BANK = (0, 1), (2, 3), (4, 5), (6, 7, 0, 1, 6, 7, 2, 3)

        x_loaded = [sem(f"x_loaded{j}") for j in range(NJ)]
        wm_loaded, w1_loaded, w2_loaded = sem("wm_loaded"), sem("w1_loaded"), sem("w2_loaded")
        b1_loaded, b2_loaded, wp_loaded, v_loaded = sem("b1_loaded"), sem("b2_loaded"), sem("wp_loaded"), sem("v_loaded")
        out_stored = sem("out_stored")
        zeroed, ident_ready = sem("zeroed"), sem("ident_ready")
        bn_done, mv_ready, sd_ready = sem("bn_done"), sem("mv_ready"), sem("sd_ready")
        rstd_ready, nmr_ready, xn_ready = sem("rstd_ready"), sem("nmr_ready"), sem("xn_ready")
        xn_dve_ready = sem("xn_dve_ready")
        ms_step, floor_ready, resid_ready = sem("ms_step"), sem("floor_ready"), sem("resid_ready")
        resid_half = sem("resid_half")
        xT_done, xT_ready, hi_ready, lo_ready = sem("xT_done"), sem("xT_ready"), sem("hi_ready"), sem("lo_ready")
        m_done, sq_ready = sem("m_done"), sem("sq_ready")
        nsq_step, nsq_ready, rsqrt_step = sem("nsq_step"), sem("nsq_ready"), sem("rsqrt_step")
        winv_ready, mn_ready = sem("winv_ready"), sem("mn_ready")
        mt_done, mt_ready = sem("mt_done"), sem("mt_ready")
        prod_ready, state_ready = sem("prod_ready"), sem("state_ready")
        seg_step, h_ready = sem("seg_step"), sem("h_ready")
        f1_done, gelu_ready = sem("f1_done"), sem("gelu_ready")
        y_done, y_ready = sem("y_done"), sem("y_ready")
        w1hi_ready, w1_ready = sem("w1hi_ready"), sem("w1_ready")
        bd_zeroed, bd_ready = sem("bd_zeroed"), sem("bd_ready")
        hs_ready, hr_ready = sem("hs_ready"), [sem(f"hr_ready{b}") for b in range(NB)]
        var_ready, last_h_ready = sem("var_ready"), sem("last_h_ready")
        start_ready, lp_ready, lp_pool_ready = sem("start_ready"), sem("lp_ready"), sem("lp_pool_ready")

        LN_RUNS = [slice(0, 1), slice(1, 2), slice(2, 4), slice(4, NJ)]
        RUN_OF = (0, 1, 2, 2, 3, 3, 3, 3)
        DVE_XN, POOL_XN = (0, 1, 2), (3, 4, 5, 6, 7)

        block = ctx.enter_context(nc.Block())

        def wait_xn(eng, j, g=G - 1):
            if j in DVE_XN:
                eng.wait_ge(xn_dve_ready, G * DVE_XN.index(j) + g + 1)
            else:
                eng.wait_ge(xn_ready, POOL_XN.index(j) + 1)

        def o_bank(j, g2):
            return ps[F_BANK[0] if (j, g2) == (NJ - 1, 1) else O_BANK[j]]

        def wait_h(eng, b):
            if b == NB - 1:
                eng.wait_ge(last_h_ready, 1)
            else:
                eng.wait_ge(h_ready, b + 1)

        @block.sync
        def _(sp):
            for j in range(NJ):
                sp.dma_start(x_sb[:, j], x_v[j // NT, j % NT]).then_inc(x_loaded[j], 16)
                if j == 1:
                    sp.dma_start(wmT[:, :], W_m).then_inc(wm_loaded, 16)
                    sp.dma_start(w1_sb[:, :], w1).then_inc(w1_loaded, 16)
                if j == 3:
                    sp.dma_start(b1_sb[:, :], b1).then_inc(b1_loaded, 16)
            sp.dma_start(b2_sb[:, :], b2.rearrange("(a d) -> a d", a=1).broadcast_to([P, D])).then_inc(b2_loaded, 16)
            sp.dma_start(w2_sb[:, :, :], w2.rearrange("(c p) e -> p c e", p=P)).then_inc(w2_loaded, 16)
            sp.dma_start(osc_sb[:, :], out_scale.rearrange("(a d) -> a d", a=1).broadcast_to([P, D])
                         ).then_inc(wp_loaded, 16)
            for g in range(G):
                i, q = g // 2, g % 2
                sp.dma_start(wp_rep[g * K:(g + 1) * K, :], W_proj[:, i]).then_inc(wp_loaded, 16)
                sp.dma_start(v_sb[g * K:(g + 1) * K, :], v_vec.rearrange("k i a -> k (i a)")).then_inc(v_loaded, 16)

            def remap_h(b):
                wait_h(sp, b)
                for i in range(2):
                    sp.dma_start(hr[64 * i:64 * i + 64, b, 0], h[0:64, b, i]).then_inc(hr_ready[b], 16)

            def store(j):
                sp.wait_ge(y_ready, j + 1)
                sp.dma_start(out_v[j // NT, j % NT], x_sb[:, j]).then_inc(out_stored, 16)

            remap_h(0)
            remap_h(1)
            store(0)
            store(1)
            remap_h(2)
            remap_h(3)
            store(2)
            store(3)
            store(4)
            store(5)
            store(6)
            for half in range(2):
                gs = slice(2 * half, 2 * half + 2)
                sp.wait_ge(y_ready, NJ + half)
                sp.dma_start(out_v[(NJ - 1) // NT, (NJ - 1) % NT][:, gs], x_sb[:, NJ - 1, gs]).then_inc(out_stored, 16)
            sp.wait_ge(out_stored, 16 * (NJ + 1))

        @block.gpsimd
        def _(pool):
            nc.gpsimd.memset(ident[:, :], 0.0).then_inc(zeroed, 1)
            pool.wait_ge(zeroed, 1)
            nc.gpsimd.affine_select(out=ident[:, :], in_=ident[:, :], compare_op=ALU.not_equal, fill=1.0, base=0,
                                    pattern=[[-1, P]], channel_multiplier=1).then_inc(ident_ready, 1)
            nc.gpsimd.memset(wp_bd[:, :, :], 0.0).then_inc(bd_zeroed, 1)

            def floors(js, step):
                pool.wait_ge(rstd_ready, RUN_OF[js.start + 1] + 1)
                nc.gpsimd.tensor_tensor(ms_a[:, js], mv[:, js, :, 1], rstd[:, js], ALU.mult).then_inc(ms_step, 1)
                pool.wait_ge(ms_step, 2 * step + 1)
                nc.gpsimd.tensor_tensor(ms_b[:, js], ms_a[:, js], rstd[:, js], ALU.mult).then_inc(ms_step, 1)
                pool.wait_ge(ms_step, 2 * step + 2)
                nc.gpsimd.tensor_scalar(floor[:, js], ms_b[:, js], NORM_FLOOR * NORM_FLOOR,
                                        RMS_EPS * NORM_FLOOR * NORM_FLOOR, ALU.mult, ALU.add).then_inc(floor_ready, 1)

            def low_part(j):
                pool.wait_ge(xT_ready, j + 1)
                pool.wait_ge(hi_ready, j + 1)
                if j >= 4:
                    pool.wait_ge(f1_done, HC * (j - 3))
                nc.gpsimd.tensor_tensor(xT_lo[:, j % 4], xT[:, j % 4], xT_hi[:, j % 4].bitcast(F32),
                                        ALU.subtract).then_inc(lo_ready, 1)

            def normalise_x(j):
                pool.wait_ge(rstd_ready, RUN_OF[j] + 1)
                pool.wait_ge(nmr_ready, RUN_OF[j] + 1)
                for g in range(G):
                    last = nc.gpsimd.tensor_scalar(xn[:, j, g], x_sb[:, j, g], rstd[:, j, g:g + 1],
                                                   nmr[:, j, g:g + 1], ALU.mult, ALU.add)
                last.then_inc(xn_ready, 1)

            def residual(j):
                wait_xn(pool, j)
                nc.gpsimd.tensor_tensor(x_sb[:, j], x_sb[:, j], xn[:, j], ALU.add).then_inc(resid_half, 1)

            def add_b2(j):
                pool.wait_ge(resid_half, j + 1)
                nc.gpsimd.tensor_tensor(x_sb[:, j], x_sb[:, j], b2_sb[:, :].unsqueeze(1).broadcast_to([P, G, D]),
                                        ALU.add).then_inc(resid_ready, 1)

            def last_of_h(b):
                lp = MT[:, b].rearrange("p l a s -> p (l a s)").rearrange("p (c l r s) -> p c l r s", c=2, l=L, r=2)
                pool.wait_ge(start_ready, b + 1)
                nc.gpsimd.tensor_tensor(lp[:, 1], ST[:, b, :, 1],
                                        HS[:, b, 1].unsqueeze(1).unsqueeze(1).broadcast_to([P, L, 2, S]),
                                        ALU.mult).then_inc(lp_pool_ready, 1)
                pool.wait_ge(lp_pool_ready, b + 1)
                pool.wait_ge(lp_ready, b + 1)
                nc.gpsimd.tensor_tensor(h[:, b].rearrange("p i (c l) -> p l i c", l=L), lp[:, 0], lp[:, 1],
                                        ALU.add).then_inc(h_ready, 1)

            pool.wait_ge(w1hi_ready, 1)
            nc.gpsimd.tensor_tensor(w1_lo[:, :], w1_sb[:, :], w1_hi[:, :].bitcast(F32),
                                    ALU.subtract).then_inc(w1_ready, 1)
            low_part(0)
            normalise_x(3)
            floors(slice(0, 2), 0)
            low_part(1)
            floors(slice(2, 4), 1)
            low_part(2)
            low_part(3)
            residual(0)
            residual(1)
            normalise_x(4)
            normalise_x(5)
            floors(slice(4, NJ), 2)
            normalise_x(6)
            normalise_x(7)
            pool.wait_ge(bd_zeroed, 1)
            pool.wait_ge(wp_loaded, 16 * (1 + G))
            for r in range(G):
                rows = slice(r * K, (r + 1) * K)
                if r == 0:
                    pool.wait_ge(resid_half, 2)
                else:
                    pool.wait_ge(bd_ready, r)
                nc.gpsimd.tensor_tensor(wp_bd[rows, r % 2], wp_rep[rows, :], osc_sb[rows, :],
                                        ALU.mult).then_inc(bd_ready, 1)
            pool.wait_ge(bd_ready, G)
            low_part(4)
            low_part(5)
            residual(2)
            residual(3)
            last_of_h(0)
            low_part(6)
            low_part(7)
            pool.wait_ge(b2_loaded, 16)
            add_b2(0)
            add_b2(1)
            residual(4)
            last_of_h(1)
            residual(5)
            add_b2(2)
            add_b2(3)
            last_of_h(2)
            residual(6)
            residual(7)
            for j in range(4, NJ):
                add_b2(j)

        @block.scalar
        def _(act):
            def std_dev(run):
                act.wait_ge(mv_ready, run + 1)
                js = LN_RUNS[run]
                nc.scalar.activation(sd[:, js], mv[:, js, :, 1], ACT.Sqrt, bias=LN_EPS).then_inc(sd_ready, 1)

            def take_xT(j):
                act.wait_ge(xT_done, j + 1)
                if j >= 4:
                    act.wait_ge(m_done, j - 3)
                    act.wait_ge(lo_ready, j - 3)
                nc.scalar.copy(xT[:, j % 4], ps[T_BANK[j % 2]][:, :]).then_inc(xT_ready, 1)
                if j >= 4:
                    act.wait_ge(f1_done, HC * (j - 3))
                nc.scalar.copy(xT_hi[:, j % 4], ps[T_BANK[j % 2]][:, :]).then_inc(hi_ready, 1)

            def squares(j):
                act.wait_ge(m_done, j + 1)
                if j >= 2:
                    act.wait_ge(nsq_step, 2 * (j // 2) - 1)
                nc.scalar.activation(sq[:, j % 2], ps[M_BANK[j % 2]][:, :], ACT.Square).then_inc(sq_ready, 1)

            def take_MT(j):
                lane = (j % NT) * CT
                act.wait_ge(mt_done, j + 1)
                src = ps[M_BANK[j % 2]][:, :].rearrange("p (a c l) -> p a l c", a=IJ, l=L)
                dst = MT[:, j // NT, :, :, lane:lane + CT].rearrange("p l a c -> p a l c")
                nc.scalar.copy(dst, src).then_inc(mt_ready, 1)

            def gelus(j, blocks=range(HC)):
                for c in blocks:
                    act.wait_ge(f1_done, HC * j + c + 1)
                    nc.scalar.activation(g_sb[:, c, j], ps[F_BANK[c % 2]][:, :], ACT.Gelu,
                                         bias=b1_sb[:, c:c + 1]).then_inc(gelu_ready, 1)

            def remap_h(b):
                wait_h(act, b)
                for i in range(2):
                    act.dma_start(hr[64 * i:64 * i + 64, b, 1], h[64:128, b, i]).then_inc(hr_ready[b], 16)

            std_dev(0)
            act.wait_ge(w1_loaded, 16)
            nc.scalar.copy(w1_hi[:, :], w1_sb[:, :]).then_inc(w1hi_ready, 1)
            std_dev(1)
            take_xT(0)
            take_xT(1)
            std_dev(2)
            squares(0)
            squares(1)
            act.wait_ge(b1_loaded, 16)
            gelus(0, (0, 1))
            take_xT(2)
            take_xT(3)
            gelus(0, (2, 3))
            gelus(1, (0, 1, 2))
            take_MT(0)
            take_MT(1)
            gelus(1, (3,))
            squares(2)
            squares(3)
            gelus(2, (0, 1))
            take_xT(4)
            gelus(2, (2, 3))
            take_xT(5)
            gelus(3, (0,))
            take_MT(2)
            take_MT(3)
            gelus(3, (1,))
            squares(4)
            squares(5)
            gelus(3, (2, 3))
            take_xT(6)
            gelus(4, (0, 1))
            take_xT(7)
            gelus(4, (2, 3))
            take_MT(4)
            take_MT(5)
            gelus(5, (0,))
            squares(6)
            squares(7)
            gelus(5, (1, 2, 3))
            remap_h(0)
            take_MT(6)
            take_MT(7)
            gelus(6)
            remap_h(1)
            gelus(7)
            remap_h(2)
            remap_h(3)

        @block.tensor
        def _(pe):
            def transpose_x(j):
                if j >= 2:
                    pe.wait_ge(xT_ready, j - 1)
                    pe.wait_ge(hi_ready, j - 1)
                for g in range(G):
                    wait_xn(pe, j, g)
                    mm = nc.tensor.transpose(ps[T_BANK[j % 2]][:, g * P:(g + 1) * P], xn[:, j, g, :], ident[:, :])
                mm.then_inc(xT_done, 1)

            def matrices(j):
                pe.wait_ge(xT_ready, j + 1)
                if j == 0:
                    pe.wait_ge(wm_loaded, 16)
                if j >= 2:
                    pe.wait_ge(mt_ready, j - 1)
                for g in range(G):
                    mm = nc.tensor.matmul(ps[M_BANK[j % 2]][:, g * P:(g + 1) * P], xT[:, j % 4, g * P:(g + 1) * P],
                                          wmT[:, :], start=True, stop=True)
                mm.then_inc(m_done, 1)

            def transpose_M(j):
                pe.wait_ge(mn_ready, j + 1)
                for a in range(IJ):
                    mm = nc.tensor.transpose(ps[M_BANK[j % 2]][:, a * P:(a + 1) * P], Mn[:, j % 2, a], ident[:, :])
                mm.then_inc(mt_done, 1)

            def ffn_in(j, blocks=range(HC)):
                if j == 0:
                    pe.wait_ge(w1_ready, 1)
                pe.wait_ge(hi_ready, j + 1)
                for c in blocks:
                    if HC * j + c >= 2:
                        pe.wait_ge(gelu_ready, HC * j + c - 1)
                    bank, cols = ps[F_BANK[c % 2]], slice(c * P, (c + 1) * P)
                    nc.tensor.matmul(bank[:, :], w1_hi[:, cols], xT_hi[:, j % 4], start=True, stop=False)
                    nc.tensor.matmul(bank[:, :], w1_lo[:, cols], xT_hi[:, j % 4], start=False, stop=False)
                    if c == 0:
                        pe.wait_ge(lo_ready, j + 1)
                    nc.tensor.matmul(bank[:, :], w1_hi[:, cols], xT_lo[:, j % 4], start=False,
                                     stop=True).then_inc(f1_done, 1)

            def ffn_out(j, blocks=range(HC)):
                if j == 0:
                    pe.wait_ge(w2_loaded, 16)
                if j == NJ - 1 and 0 in blocks:
                    pe.wait_ge(gelu_ready, HC * NJ)
                if j in (2, 3) and 0 in blocks:
                    pe.wait_ge(xT_ready, j + 5)
                    pe.wait_ge(hi_ready, j + 5)
                if j in (4, 5) and 0 in blocks:
                    pe.wait_ge(y_ready, j - 3)
                if j in (6, 7) and 0 in blocks:
                    pe.wait_ge(mt_ready, j + 1)
                for c in blocks:
                    pe.wait_ge(gelu_ready, HC * j + c + 1)
                    for g in range(G):
                        last = (j, c) == (NJ - 1, HC - 1)
                        first = c == 0 and (g == 0 or (g == 2 and j == NJ - 1))
                        mm = nc.tensor.matmul(o_bank(j, g // 2)[:, g * D:(g + 1) * D],
                                              g_sb[:, c, j, g * P:(g + 1) * P], w2_sb[:, c], start=first, stop=last,
                                              skip_group_check=True)
                        if last and g % 2 == 1:
                            mm.then_inc(y_done, 1)

            def project(j):
                b, tok = j // NT, slice((j % NT) * P, (j % NT + 1) * P)
                pe.wait_ge(hr_ready[b], 16 * 4)
                if j == 0:
                    pe.wait_ge(bd_ready, G)
                for g2 in range(2):
                    mm = nc.tensor.matmul(o_bank(j, g2)[:, g2 * 2 * D:(g2 + 1) * 2 * D], hr[:, b, g2, tok],
                                          wp_bd[:, :, :], start=False, stop=(j < NJ - 1), skip_group_check=True)
                if j < NJ - 1:
                    mm.then_inc(y_done, 1)

            pe.wait_ge(ident_ready, 1)
            for _ in range(WARM_UP):
                nc.tensor.matmul(ps[F_BANK[0]][:, 0:P], ident[:, :], ident[:, :], start=True, stop=True)
            transpose_x(0)
            transpose_x(1)
            matrices(0)
            matrices(1)
            ffn_in(0, (0, 1))
            transpose_x(2)
            transpose_x(3)
            ffn_in(0, (2, 3))
            ffn_out(0, (0, 1))
            ffn_in(1, (0, 1))
            ffn_out(0, (2,))
            ffn_in(1, (2,))
            transpose_M(0)
            transpose_M(1)
            ffn_in(1, (3,))
            matrices(2)
            matrices(3)
            ffn_out(0, (3,))
            ffn_in(2, (0, 1))
            ffn_out(1, (0, 1))
            transpose_x(4)
            ffn_in(2, (2, 3))
            ffn_out(1, (2,))
            transpose_x(5)
            ffn_in(3, (0,))
            transpose_M(2)
            transpose_M(3)
            ffn_in(3, (1,))
            matrices(4)
            matrices(5)
            ffn_out(1, (3,))
            ffn_in(3, (2, 3))
            transpose_x(6)
            ffn_in(4, (0, 1))
            transpose_x(7)
            ffn_in(4, (2, 3))
            ffn_out(2, (0, 1))
            transpose_M(4)
            transpose_M(5)
            ffn_in(5, (0,))
            matrices(6)
            matrices(7)
            ffn_in(5, (1,))
            ffn_out(2, (2, 3))
            ffn_in(5, (2, 3))
            ffn_out(3)
            project(0)
            project(1)
            transpose_M(6)
            transpose_M(7)
            ffn_in(6, (0, 1))
            ffn_out(4, (0, 1))
            ffn_in(6, (2, 3))
            ffn_out(4, (2, 3))
            ffn_in(7, (0, 1))
            ffn_out(5, (0, 1))
            ffn_in(7, (2, 3))
            ffn_out(5, (2, 3))
            project(2)
            project(3)
            ffn_out(6)
            ffn_out(7, (0, 1))
            project(4)
            project(5)
            ffn_out(7, (2,))
            project(6)
            project(7)
            ffn_out(7, (3,))

        @block.vector
        def _(dve):
            steps = {"seg": 0, "prod": 0, "state": 0, "rsqrt": 0}

            def counted(name, sem, ins):
                ins.then_inc(sem, 1)
                steps[name] += 1
                return steps[name]

            def nothing():
                pass

            def moments(run):
                chunks = range(LN_RUNS[run].start, LN_RUNS[run].stop)
                for j in chunks:
                    dve.wait_ge(x_loaded[j], 16)
                    for g in range(G):
                        nc.vector.bn_stats(stats[:, j, g], x_sb[:, j, g]).then_inc(bn_done, 1)
                        yield
                for j in chunks:
                    for g in range(G):
                        dve.wait_ge(bn_done, G * j + g + 1)
                        last = nc.vector.bn_aggr(mv[:, j, g], stats[:, j, g])
                        if (j, g) == (chunks[-1], G - 1):
                            last.then_inc(mv_ready, 1)
                        yield

            def layernorm_scale(run):
                js = LN_RUNS[run]
                dve.wait_ge(sd_ready, run + 1)
                nc.vector.reciprocal(rstd[:, js], sd[:, js]).then_inc(rstd_ready, 1)
                dve.wait_ge(rstd_ready, run + 1)
                nc.vector.scalar_tensor_tensor(nmr[:, js], mv[:, js, :, 0], -1.0, rstd[:, js],
                                               ALU.mult, ALU.mult).then_inc(nmr_ready, 1)

            def normalise_x(j):
                for g in range(G):
                    nc.vector.tensor_scalar(xn[:, j, g], x_sb[:, j, g], rstd[:, j, g:g + 1], nmr[:, j, g:g + 1],
                                            ALU.mult, ALU.add).then_inc(xn_dve_ready, 1)

            def squared_norms(p, tick):
                s4 = sq[:, :, :, :, :].rearrange("p j g a k -> p (j g) a k")
                dve.wait_ge(sq_ready, 2 * p + 2)
                nc.vector.tensor_tensor(sq2[:, :, :, :], s4[:, :, 0:2], s4[:, :, 2:4], ALU.add).then_inc(nsq_step, 1)
                tick()
                dve.wait_ge(nsq_step, 2 * p + 1)
                nc.vector.tensor_tensor(nsq0[:, :, :], sq2[:, :, 0], sq2[:, :, 1], ALU.add).then_inc(nsq_step, 1)
                tick()
                dve.wait_ge(nsq_step, 2 * p + 2)
                dve.wait_ge(floor_ready, min(p, 2) + 1)
                fl = floor[:, 2 * p:2 * p + 2].rearrange("p j g -> p (j g)").unsqueeze(2).broadcast_to([P, 2 * G, K])
                nc.vector.tensor_tensor(nsq[:, :, :], nsq0[:, :, :], fl, ALU.max).then_inc(nsq_ready, 1)
                tick()

            def rsqrt(src, out, y0, y1, t0, t1, tick):
                n = counted("rsqrt", rsqrt_step, nc.vector.tensor_scalar(
                    y0.bitcast(mybir.dt.int32), src.bitcast(mybir.dt.int32), -0.5, RSQRT_MAGIC, ALU.mult, ALU.add))
                tick()
                for y, nxt, a, b in ((y0, y1, RSQRT_A, RSQRT_B), (y1, out, 0.5, RSQRT_C)):
                    dve.wait_ge(rsqrt_step, n)
                    n = counted("rsqrt", rsqrt_step,
                                nc.vector.scalar_tensor_tensor(t0, y, -a, y, ALU.mult, ALU.mult))
                    tick()
                    dve.wait_ge(rsqrt_step, n)
                    n = counted("rsqrt", rsqrt_step, nc.vector.tensor_tensor(t1, t0, src, ALU.mult))
                    tick()
                    dve.wait_ge(rsqrt_step, n)
                    last = nc.vector.scalar_tensor_tensor(nxt, t1, b, y, ALU.add, ALU.mult)
                    if nxt is y1:
                        n = counted("rsqrt", rsqrt_step, last)
                        tick()
                return last

            def inverse_norms(p, tick):
                dve.wait_ge(nsq_ready, p + 1)
                rsqrt(nsq[:, :, :], winv[:, :, :, :].rearrange("p j g k -> p (j g) k"), ry[:, :, :], ry1[:, :, :],
                      ra[:, :, :], rb[:, :, :], tick).then_inc(winv_ready, 1)
                tick()

            def late_scales(tick):
                js = slice(4, NJ)
                nc.vector.tensor_scalar(vv[:, 0], mv[:, js, :, 1].rearrange("p j g -> p (j g)"), LN_EPS, None,
                                        ALU.add).then_inc(var_ready, 1)
                tick()
                dve.wait_ge(var_ready, 1)
                rsqrt(vv[:, 0], rstd[:, js].rearrange("p j g -> p (j g)"), lv[:, 0], lv[:, 1], lv[:, 2], lv[:, 3],
                      tick).then_inc(rstd_ready, 1)
                tick()
                dve.wait_ge(rstd_ready, 4)
                nc.vector.scalar_tensor_tensor(nmr[:, js], mv[:, js, :, 0], -1.0, rstd[:, js],
                                               ALU.mult, ALU.mult).then_inc(nmr_ready, 1)
                tick()

            def normalise_M(p, tick):
                dve.wait_ge(winv_ready, p + 1)
                for j in (2 * p, 2 * p + 1):
                    if j >= 2:
                        dve.wait_ge(mt_done, j - 1)
                    src = ps[M_BANK[j % 2]][:, :].rearrange("p (g a k) -> p a g k", g=G, a=IJ)
                    w = winv[:, j % 2].unsqueeze(1).broadcast_to([P, IJ, G, K])
                    nc.vector.tensor_tensor(Mn[:, j % 2], src, w, ALU.mult).then_inc(mn_ready, 1)
                    tick()

            def compose(dst, tmp, later, earlier):
                n = dst.shape[-1]
                for k in range(2):
                    done = counted("seg", seg_step, nc.vector.tensor_tensor(
                        tmp[:, k, :, :, 0:n], later[:, k].unsqueeze(1).broadcast_to([P, 2, 2, n]),
                        earlier[:, :, k].unsqueeze(2).broadcast_to([P, 2, 2, n]), ALU.mult))
                    yield
                dve.wait_ge(seg_step, done)
                done = counted("seg", seg_step, nc.vector.tensor_tensor(dst, tmp[:, 0, :, :, 0:n],
                                                                        tmp[:, 1, :, :, 0:n], ALU.add))
                yield
                dve.wait_ge(seg_step, done)

            def carry(dst, tmp, mat, vec, final=None):
                n = dst.shape[-1]
                done = counted("seg", seg_step, nc.vector.tensor_tensor(
                    tmp[:, :, :, 0:n], mat, vec.unsqueeze(2).broadcast_to([P, 2, 2, n]), ALU.mult))
                yield
                dve.wait_ge(seg_step, done)
                last = nc.vector.tensor_tensor(dst, tmp[:, 0, :, 0:n], tmp[:, 1, :, 0:n], ALU.add)
                if final is None:
                    done = counted("seg", seg_step, last)
                    yield
                    dve.wait_ge(seg_step, done)
                else:
                    last.then_inc(start_ready, 1)
                    yield
                    dve.wait_ge(start_ready, final)

            def scan(b):
                dve.wait_ge(mt_ready, NT * (b + 1))
                state = counted("state", state_ready, nc.vector.tensor_copy(
                    ST[:, b, 0], MT[:, b, 0].rearrange("p (i c) s -> p c i s", i=2)))
                yield
                for l in range(1, L):
                    pr = PR[:, b % 2]
                    m = MT[:, b, l].rearrange("p (i k) s -> p i (k s)", i=2)
                    st = ST[:, b, l - 1].rearrange("p c k s -> p c (k s)")
                    dve.wait_ge(state_ready, state)
                    prod = counted("prod", prod_ready, nc.vector.tensor_tensor(
                        pr.rearrange("p i c k s -> p i c (k s)"), m.unsqueeze(2).broadcast_to([P, 2, 2, 2 * S]),
                        st.unsqueeze(1).broadcast_to([P, 2, 2, 2 * S]), ALU.mult))
                    yield
                    dve.wait_ge(prod_ready, prod)
                    state = counted("state", state_ready, nc.vector.tensor_tensor(
                        ST[:, b, l].rearrange("p c i s -> p i c s"), pr[:, :, :, 0], pr[:, :, :, 1], ALU.add))
                    yield
                tot, hs = ST[:, b, L - 1], HS[:, b]
                s2, s4, s8, cp, hp = SEG2[:, b % 2], SEG4[:, b % 2], SEG8[:, b % 2], CP[:, b % 2], HP[:, b % 2]
                dve.wait_ge(state_ready, state)
                yield from compose(s2, cp, tot[:, :, :, 1::2], tot[:, :, :, 0::2])
                yield from compose(s4, cp, s2[:, :, :, 1::2], s2[:, :, :, 0::2])
                yield from compose(s8, cp, s4[:, :, :, 1::2], s4[:, :, :, 0::2])
                if b == 0:
                    dve.wait_ge(hs_ready, 1)
                for q in range(S // 8 - 1):
                    yield from carry(hs[:, :, 8 * q + 8:8 * q + 9], hp, s8[:, :, :, q:q + 1],
                                     hs[:, :, 8 * q:8 * q + 1])
                yield from carry(hs[:, :, 4::8], hp, s4[:, :, :, 0::2], hs[:, :, 0::8])
                yield from carry(hs[:, :, 2::4], hp, s2[:, :, :, 0::2], hs[:, :, 0::4])
                yield from carry(hs[:, :, 1::2], hp, tot[:, :, :, 0::2], hs[:, :, 0::2], b + 1)
                lp = MT[:, b].rearrange("p l a s -> p (l a s)").rearrange("p (c l r s) -> p c l r s", c=2, l=L, r=2)
                for c in range(2 if b == NB - 1 else 1):
                    last = nc.vector.tensor_tensor(
                        lp[:, c], ST[:, b, :, c],
                        hs[:, c].unsqueeze(1).unsqueeze(1).broadcast_to([P, L, 2, S]), ALU.mult)
                    if b < NB - 1:
                        last.then_inc(lp_ready, 1)
                    else:
                        done = counted("seg", seg_step, last)
                    yield
                if b == NB - 1:
                    dve.wait_ge(seg_step, done)
                    nc.vector.tensor_tensor(h[:, b].rearrange("p i (c l) -> p l i c", l=L), lp[:, 0], lp[:, 1],
                                            ALU.add).then_inc(last_h_ready, 1)
                    yield

            def last_output():
                for half in range(2):
                    gs, cols = slice(2 * half, 2 * half + 2), slice(2 * half * D, 2 * (half + 1) * D)
                    dve.wait_ge(y_done, NJ + half)
                    dve.wait_ge(resid_ready, NJ)
                    nc.vector.tensor_tensor(x_sb[:, NJ - 1, gs].rearrange("p g d -> p (g d)"),
                                            o_bank(NJ - 1, half)[:, cols],
                                            x_sb[:, NJ - 1, gs].rearrange("p g d -> p (g d)"),
                                            ALU.add).then_inc(y_ready, 1)

            def output(j):
                dve.wait_ge(y_done, j + 1)
                dve.wait_ge(resid_ready, j + 1)
                nc.vector.tensor_tensor(x_sb[:, j].rearrange("p g d -> p (g d)"), ps[O_BANK[j]][:, :],
                                        x_sb[:, j].rearrange("p g d -> p (g d)"), ALU.add).then_inc(y_ready, 1)

            def run_all(steps):
                for _ in steps:
                    pass

            moments_1 = moments(1)
            run_all(moments(0))
            run_all(itertools.islice(moments_1, G))
            layernorm_scale(0)
            run_all(moments_1)
            dve.wait_ge(nmr_ready, 1)
            normalise_x(0)
            layernorm_scale(1)
            dve.wait_ge(nmr_ready, 2)
            normalise_x(1)
            run_all(moments(2))
            layernorm_scale(2)
            dve.wait_ge(nmr_ready, 3)
            normalise_x(2)
            late = moments(3)

            def tick():
                next(late, None)
                next(late, None)

            squared_norms(0, tick)
            inverse_norms(0, tick)
            normalise_M(0, nothing)
            run_all(late)
            dve.wait_ge(mv_ready, 4)
            dve.wait_ge(v_loaded, 16 * G)
            nc.vector.tensor_copy(HS[:, :, :, 0], v_sb[:, :].unsqueeze(1).broadcast_to([P, NB, 2])).then_inc(hs_ready, 1)
            scans = [scan(b) for b in range(NB)]

            DONE = "done"

            TICKS = (11, 11, 11)

            def take(b, n):
                for _ in range(n):
                    next(scans[b], None)

            def alternate(n):
                for _ in range(n):
                    take(active[0], 1)
                    take(active[1], 1)

            def to_matrices(p, ticks):
                spent = [0, 0]

                def tick():
                    spent[0] += 1
                    if spent[0] * ticks // 11 > spent[1]:
                        spent[1] += 1
                        if p == 1 or next(scans[p - 2], DONE) is DONE:
                            take(p - 1, 1)

                squared_norms(p, tick)
                inverse_norms(p, tick)
                normalise_M(p, tick)

            late_scales(lambda: take(0, 1))
            to_matrices(1, TICKS[0])
            take(0, 6)
            active = (0, 1)
            alternate(4)
            to_matrices(2, TICKS[1])
            run_all(scans[0])
            take(1, 6)
            active = (1, 2)
            alternate(4)
            to_matrices(3, TICKS[2])
            run_all(scans[1])
            output(0)
            output(1)
            take(2, 2)
            active = (2, 3)
            alternate(20)
            run_all(scans[2])
            run_all(scans[3])
            for j in range(2, NJ - 1):
                output(j)
            last_output()


_INS = ['L0_attn_x', 'L0_attn_W_m', 'L0_attn_v_vec', 'L0_attn_W_proj', 'L0_attn_out_scale',
        'L0_ffn_w1', 'L0_ffn_b1', 'L0_ffn_w2', 'L0_ffn_b2']
_OUTS = [((16, 256, 128), 'float32')]


def kernel(**inputs):
    import numpy as _np
    import concourse.bacc as _bacc
    from concourse import mybir as _mybir
    from concourse.bass_utils import run_bass_kernel_spmd as _run

    nc = _bacc.Bacc("TRN2", target_bir_lowering=False, num_devices=1)
    laid = dict(inputs)
    laid['L0_attn_W_m'] = _np.asarray(inputs['L0_attn_W_m']).reshape(32, 4, 128).transpose(2, 1, 0).reshape(128, 128)
    laid['L0_attn_W_proj'] = _np.asarray(inputs['L0_attn_W_proj']).reshape(128, 32, 2).transpose(1, 2, 0)
    laid['L0_ffn_b1'] = _np.asarray(inputs['L0_ffn_b1']).reshape(4, 128).T
    arrays, args = {}, []
    for name in _INS:
        a = _np.ascontiguousarray(laid[name])
        arrays[f"in_{name}_dram"] = a
        args.append(nc.dram_tensor(f"in_{name}_dram", a.shape, _mybir.dt.from_np(a.dtype), kind="ExternalInput").ap())
    for i, (shape, dtype) in enumerate(_OUTS):
        dt = _mybir.dt.from_np(_np.dtype(dtype))
        args.append(nc.dram_tensor(f"out_{i}_dram", shape, dt, kind="ExternalOutput").ap())
    block_kernel(nc, *args)
    r = _run(nc, [arrays], core_ids=[0])
    got = tuple(r.results[0][f"out_{i}_dram"] for i in range(len(_OUTS)))
    return got[0]
```

```python
import itertools
from contextlib import ExitStack

import concourse.bass as bass
from concourse import mybir

F32 = mybir.dt.float32
F32R = mybir.dt.float32r
ALU = mybir.AluOpType
ACT = mybir.ActivationFunctionType

LN_EPS = 1e-5
RMS_EPS = 1.1920929e-07
NORM_FLOOR = 1e-6

RSQRT_MAGIC = float(0x5F1FFFF9)
RSQRT_A, RSQRT_B = 0.703952253, 0.703952253 * 2.38924456
RSQRT_C = 1.5 + 3e-7

WARM_UP = 12


def block_kernel(nc, x, W_m, v_vec, W_proj, out_scale, w1, b1, w2, b2, out):
    B, T, D = x.shape
    K = v_vec.shape[0]
    NH = w1.shape[1]
    P = 128
    G = P // K
    NB = B // G
    NT = T // P
    NJ = NB * NT
    HC = NH // P
    IJ = 4
    CH = G * P
    L = 8
    S = T // L
    CT = P // L
    assert (P, G, NJ, D, NT) == (128, 4, 8, 128, 2) and K * G == P and S == 32

    x_v = x.rearrange("(g b) (h p) d -> b h p g d", g=G, p=P)
    out_v = out.rearrange("(g b) (h p) d -> b h p g d", g=G, p=P)

    ctx = ExitStack()
    with ctx:
        def sb(name, shape, dt=F32):
            return ctx.enter_context(nc.sbuf_tensor(name, shape, dt))

        def sem(name):
            return ctx.enter_context(nc.semaphore(name))

        ident = sb("ident", [P, P])
        wmT = sb("wmT", [P, IJ * K])
        w1_sb = sb("w1_sb", [P, NH])
        w1_hi = sb("w1_hi", [P, NH], F32R)
        w1_lo = sb("w1_lo", [P, NH], F32R)
        w2_sb = sb("w2_sb", [P, HC, D])
        b1_sb = sb("b1_sb", [P, HC])
        b2_sb = sb("b2_sb", [P, D])
        wp_rep = sb("wp_rep", [P, D])
        osc_sb = sb("osc_sb", [P, D])
        wp_bd = sb("wp_bd", [P, 2, D])
        wp_hi = sb("wp_hi", [P, 2, D], F32R)
        wp_lo = sb("wp_lo", [P, 2, D], F32R)
        v_sb = sb("v_sb", [P, 2])

        x_sb = sb("x_sb", [P, NJ, G, D])
        xn = sb("xn", [P, NJ, G, D])
        stats = sb("stats", [P, NJ, G, 6])
        mv = sb("mv", [P, NJ, G, 2])
        sd = sb("sd", [P, NJ, G])
        rstd = sb("rstd", [P, NJ, G])
        nmr = sb("nmr", [P, NJ, G])
        ms_a = sb("ms_a", [P, NJ, G])
        ms_b = sb("ms_b", [P, NJ, G])
        floor = sb("floor", [P, NJ, G])
        xT = sb("xT", [P, 4, CH])
        xT_hi = sb("xT_hi", [P, 4, CH], F32R)
        xT_lo = sb("xT_lo", [P, 4, CH], F32R)
        sq = sb("sq", [P, 2, G, IJ, K])
        sq2 = sb("sq2", [P, 2 * G, 2, K])
        nsq = sb("nsq", [P, 2 * G, K])
        vv = sb("vv", [P, 4 * G])
        lv = sb("lv", [P, 4, 4 * G])
        ra = sb("ra", [P, 2 * G, K])
        ry, ry1, nsq0 = sq2[:, :, 0], sq2[:, :, 1], ra
        rb = sb("rb", [P, 2 * G, K])
        winv = sb("winv", [P, 2, G, K])
        Mn = sb("Mn", [P, 2, IJ, G, K])
        MT = sb("MT", [P, NB, L, IJ, S])
        ST = sb("ST", [P, NB, L, 2, 2, S])
        PR = sb("PR", [P, 2, 2, 2, 2, S])
        CP = sb("CP", [P, 2, 2, 2, 2, S // 2])
        SEG2 = sb("SEG2", [P, 2, 2, 2, S // 2])
        SEG4 = sb("SEG4", [P, 2, 2, 2, S // 4])
        SEG8 = sb("SEG8", [P, 2, 2, 2, S // 8])
        HP = sb("HP", [P, 2, 2, 2, S // 2])
        HS = sb("HS", [P, NB, 2, S])
        h = sb("h", [P, NB, 2, T])
        hr = sb("hr", [P, NB, 2, T])
        hr_hi = sb("hr_hi", [P, 2, T], F32R)
        hr_lo = sb("hr_lo", [P, 2, T], F32R)
        g_sb = sb("g_sb", [P, HC, NJ, CH])

        ps = [ctx.enter_context(nc.psum_tensor(f"bank{i}", [P, CH], F32)) for i in range(8)]
        T_BANK, M_BANK, F_BANK, O_BANK = (0, 1), (2, 3), (4, 5), (6, 7, 0, 1, 2, 3, 6, 5)

        x_loaded = [sem(f"x_loaded{j}") for j in range(NJ)]
        x0_loaded = sem("x0_loaded")
        wm_loaded, w1_loaded, w2_loaded = sem("wm_loaded"), sem("w1_loaded"), sem("w2_loaded")
        b1_loaded, b2_loaded, wp_loaded, v_loaded = sem("b1_loaded"), sem("b2_loaded"), sem("wp_loaded"), sem("v_loaded")
        out_stored = sem("out_stored")
        zeroed, ident_ready = sem("zeroed"), sem("ident_ready")
        bn_done, mv_ready, sd_ready = sem("bn_done"), sem("mv_ready"), sem("sd_ready")
        rstd_ready, nmr_ready, xn_ready = sem("rstd_ready"), sem("nmr_ready"), sem("xn_ready")
        xn_dve_ready = sem("xn_dve_ready")
        ms_step, floor_ready, resid_ready = sem("ms_step"), sem("floor_ready"), sem("resid_ready")
        resid_half = sem("resid_half")
        xT_done, xT_ready, hi_ready, lo_ready = sem("xT_done"), sem("xT_ready"), sem("hi_ready"), sem("lo_ready")
        m_done, sq_ready = sem("m_done"), sem("sq_ready")
        nsq_step, nsq_ready, rsqrt_step = sem("nsq_step"), sem("nsq_ready"), sem("rsqrt_step")
        winv_ready, mn_ready = sem("winv_ready"), sem("mn_ready")
        mt_done, mt_ready = sem("mt_done"), sem("mt_ready")
        prod_ready, state_ready = sem("prod_ready"), sem("state_ready")
        seg_step, h_ready = sem("seg_step"), sem("h_ready")
        f1_done, gelu_ready = sem("f1_done"), sem("gelu_ready")
        y_done, y_ready = sem("y_done"), sem("y_ready")
        w1hi_ready, w1_ready = sem("w1hi_ready"), sem("w1_ready")
        bd_zeroed, bd_ready = sem("bd_zeroed"), sem("bd_ready")
        hs_ready, hr_copied = sem("hs_ready"), sem("hr_copied")
        wp_hi_ready, wp_lo_ready = sem("wp_hi_ready"), sem("wp_lo_ready")
        hr_hi_ready, hr_lo_ready = sem("hr_hi_ready"), sem("hr_lo_ready")
        hr_moved = [sem(f"hr_moved{b}") for b in range(NB)]
        var_ready, last_h_ready, half_ready = sem("var_ready"), sem("last_h_ready"), sem("half_ready")
        start_ready, lp_ready = sem("start_ready"), sem("lp_ready")

        POOL_H = 2
        SPLIT_H = 2
        LN_RUNS = [slice(0, 1), slice(1, 2), slice(2, 4), slice(4, NJ)]
        RUN_OF = (0, 1, 2, 2, 3, 3, 3, 3)
        DVE_XN, POOL_XN = (0, 1, 2), (3, 4, 5, 6, 7)

        block = ctx.enter_context(nc.Block())

        def wait_xn(eng, j, g=G - 1):
            if j in DVE_XN:
                eng.wait_ge(xn_dve_ready, G * DVE_XN.index(j) + g + 1)
            else:
                eng.wait_ge(xn_ready, POOL_XN.index(j) + 1)

        def o_bank(j, g2):
            return ps[F_BANK[0] if (j, g2) == (NJ - 1, 1) else O_BANK[j]]

        def f_bank(j, c):
            return ps[(F_BANK + O_BANK[:2])[c] if j == 0 else F_BANK[c % 2]]

        def lp_of(b):
            return MT[:, b].rearrange("p l a s -> p (l a s)").rearrange("p (c l r s) -> p c l r s", c=2, l=L, r=2)

        def wait_hr(eng, b):
            eng.wait_ge(hr_moved[b], 16 * 2)
            eng.wait_ge(hr_copied, 2 * (b + 1))

        def wait_h(eng, b):
            if b >= POOL_H:
                eng.wait_ge(last_h_ready, b - POOL_H + 1)
            else:
                eng.wait_ge(h_ready, b + 1)

        @block.sync
        def _(sp):
            sp.dma_start(x_sb[:, 0, 0:2], x_v[0, 0][:, 0:2]).then_inc(x0_loaded, 16)
            for j in range(NJ):
                if j > 0:
                    sp.dma_start(x_sb[:, j], x_v[j // NT, j % NT]).then_inc(x_loaded[j], 16)
                if j == 1:
                    sp.dma_start(wmT[:, :], W_m).then_inc(wm_loaded, 16)
                    sp.dma_start(w1_sb[:, :], w1).then_inc(w1_loaded, 16)
                if j == 3:
                    sp.dma_start(b1_sb[:, :], b1).then_inc(b1_loaded, 16)
            sp.dma_start(b2_sb[:, :], b2.rearrange("(a d) -> a d", a=1).broadcast_to([P, D])).then_inc(b2_loaded, 16)
            sp.dma_start(w2_sb[:, :, :], w2.rearrange("(c p) e -> p c e", p=P)).then_inc(w2_loaded, 16)
            sp.dma_start(osc_sb[:, :], out_scale.rearrange("(a d) -> a d", a=1).broadcast_to([P, D])
                         ).then_inc(wp_loaded, 16)
            for g in range(G):
                i, q = g // 2, g % 2
                sp.dma_start(wp_rep[g * K:(g + 1) * K, :], W_proj[:, i]).then_inc(wp_loaded, 16)
                sp.dma_start(v_sb[g * K:(g + 1) * K, :], v_vec.rearrange("k i a -> k (i a)")).then_inc(v_loaded, 16)

            def remap_h(b):
                wait_h(sp, b)
                sp.dma_start(hr[64:128, b, 0], h[0:64, b, 1]).then_inc(hr_moved[b], 16)

            def store(j):
                sp.wait_ge(y_ready, j + 1)
                sp.dma_start(out_v[j // NT, j % NT], x_sb[:, j]).then_inc(out_stored, 16)

            remap_h(0)
            remap_h(1)
            store(0)
            remap_h(2)
            remap_h(3)
            store(1)
            store(2)
            store(3)
            store(4)
            store(5)
            store(6)
            for half in range(2):
                gs = slice(2 * half, 2 * half + 2)
                sp.wait_ge(y_ready, NJ + half)
                sp.dma_start(out_v[(NJ - 1) // NT, (NJ - 1) % NT][:, gs], x_sb[:, NJ - 1, gs]).then_inc(out_stored, 16)
            sp.wait_ge(out_stored, 16 * (NJ + 1))

        @block.gpsimd
        def _(pool):
            nc.gpsimd.memset(ident[:, :], 0.0).then_inc(zeroed, 1)
            pool.wait_ge(zeroed, 1)
            nc.gpsimd.affine_select(out=ident[:, :], in_=ident[:, :], compare_op=ALU.not_equal, fill=1.0, base=0,
                                    pattern=[[-1, P]], channel_multiplier=1).then_inc(ident_ready, 1)
            nc.gpsimd.memset(wp_bd[:, :, :], 0.0).then_inc(bd_zeroed, 1)

            def floors(js, step):
                pool.wait_ge(rstd_ready, RUN_OF[js.start + 1] + 1)
                nc.gpsimd.tensor_tensor(ms_a[:, js], mv[:, js, :, 1], rstd[:, js], ALU.mult).then_inc(ms_step, 1)
                pool.wait_ge(ms_step, 2 * step + 1)
                nc.gpsimd.tensor_tensor(ms_b[:, js], ms_a[:, js], rstd[:, js], ALU.mult).then_inc(ms_step, 1)
                pool.wait_ge(ms_step, 2 * step + 2)
                nc.gpsimd.tensor_scalar(floor[:, js], ms_b[:, js], NORM_FLOOR * NORM_FLOOR,
                                        RMS_EPS * NORM_FLOOR * NORM_FLOOR, ALU.mult, ALU.add).then_inc(floor_ready, 1)

            def low_part(j):
                pool.wait_ge(xT_ready, j + 1)
                pool.wait_ge(hi_ready, j + 1)
                if j >= 4:
                    pool.wait_ge(f1_done, HC * (j - 3))
                nc.gpsimd.tensor_tensor(xT_lo[:, j % 4], xT[:, j % 4], xT_hi[:, j % 4].bitcast(F32),
                                        ALU.subtract).then_inc(lo_ready, 1)

            def normalise_x(j):
                pool.wait_ge(rstd_ready, RUN_OF[j] + 1)
                pool.wait_ge(nmr_ready, RUN_OF[j] + 1)
                for g in range(G):
                    last = nc.gpsimd.tensor_scalar(xn[:, j, g], x_sb[:, j, g], rstd[:, j, g:g + 1],
                                                   nmr[:, j, g:g + 1], ALU.mult, ALU.add)
                last.then_inc(xn_ready, 1)

            def residual(j):
                wait_xn(pool, j)
                nc.gpsimd.tensor_tensor(x_sb[:, j], x_sb[:, j], xn[:, j], ALU.add).then_inc(resid_half, 1)

            def add_b2(j):
                pool.wait_ge(resid_half, j + 1)
                nc.gpsimd.tensor_tensor(x_sb[:, j], x_sb[:, j], b2_sb[:, :].unsqueeze(1).broadcast_to([P, G, D]),
                                        ALU.add).then_inc(resid_ready, 1)

            def low_part_of_h(b):
                wait_hr(pool, b)
                pool.wait_ge(hr_hi_ready, b + 1)
                if b > 0:
                    pool.wait_ge(y_done, NT * b)
                nc.gpsimd.tensor_tensor(hr_lo[:, :, :], hr[:, b], hr_hi[:, :, :].bitcast(F32),
                                        ALU.subtract).then_inc(hr_lo_ready, 1)

            def product_of_h(b, c):
                pool.wait_ge(start_ready, b + 1)
                nc.gpsimd.tensor_tensor(lp_of(b)[:, c], ST[:, b, :, c],
                                        HS[:, b, c].unsqueeze(1).unsqueeze(1).broadcast_to([P, L, 2, S]),
                                        ALU.mult).then_inc(lp_ready, 1)

            def last_of_h(b):
                lp = lp_of(b)
                product_of_h(b, 0)
                product_of_h(b, 1)
                pool.wait_ge(lp_ready, 2 * (b + 1))
                nc.gpsimd.tensor_tensor(h[:, b].rearrange("p i (c l) -> p l i c", l=L), lp[:, 0], lp[:, 1],
                                        ALU.add).then_inc(h_ready, 1)

            pool.wait_ge(w1hi_ready, 1)
            nc.gpsimd.tensor_tensor(w1_lo[:, :], w1_sb[:, :], w1_hi[:, :].bitcast(F32),
                                    ALU.subtract).then_inc(w1_ready, 1)
            low_part(0)
            low_part(1)
            normalise_x(3)
            floors(slice(0, 2), 0)
            floors(slice(2, 4), 1)
            low_part(2)
            low_part(3)
            residual(0)
            residual(1)
            normalise_x(4)
            normalise_x(5)
            floors(slice(4, NJ), 2)
            normalise_x(6)
            low_part(4)
            normalise_x(7)
            low_part(5)
            residual(2)
            last_of_h(0)
            low_part(6)
            low_part(7)
            pool.wait_ge(bd_zeroed, 1)
            pool.wait_ge(wp_loaded, 16 * (1 + G))
            for r in range(G):
                rows = slice(r * K, (r + 1) * K)
                if r == 0:
                    pool.wait_ge(lo_ready, NJ)
                else:
                    pool.wait_ge(bd_ready, r)
                nc.gpsimd.tensor_tensor(wp_bd[rows, r % 2], wp_rep[rows, :], osc_sb[rows, :],
                                        ALU.mult).then_inc(bd_ready, 1)
            pool.wait_ge(bd_ready, G)
            residual(3)
            pool.wait_ge(wp_hi_ready, 1)
            nc.gpsimd.tensor_tensor(wp_lo[:, :, :], wp_bd[:, :, :], wp_hi[:, :, :].bitcast(F32),
                                    ALU.subtract).then_inc(wp_lo_ready, 1)
            low_part_of_h(0)
            pool.wait_ge(b2_loaded, 16)
            add_b2(0)
            residual(4)
            last_of_h(1)
            for j in range(5, NJ):
                residual(j)
            for j in range(1, 3):
                add_b2(j)
            product_of_h(POOL_H, 1)
            low_part_of_h(1)
            for j in range(3, NJ):
                add_b2(j)

        @block.scalar
        def _(act):
            def std_dev(run):
                act.wait_ge(mv_ready, run + 1)
                js = LN_RUNS[run]
                nc.scalar.activation(sd[:, js], mv[:, js, :, 1], ACT.Sqrt, bias=LN_EPS).then_inc(sd_ready, 1)

            def take_xT(j):
                act.wait_ge(xT_done, j + 1)
                if j >= 4:
                    act.wait_ge(m_done, j - 3)
                    act.wait_ge(lo_ready, j - 3)
                nc.scalar.copy(xT[:, j % 4], ps[T_BANK[j % 2]][:, :]).then_inc(xT_ready, 1)
                if j >= 4:
                    act.wait_ge(f1_done, HC * (j - 3))
                nc.scalar.copy(xT_hi[:, j % 4], ps[T_BANK[j % 2]][:, :]).then_inc(hi_ready, 1)

            def squares(j):
                act.wait_ge(m_done, j + 1)
                if j >= 2:
                    act.wait_ge(nsq_step, 2 * (j // 2) - 1)
                nc.scalar.activation(sq[:, j % 2], ps[M_BANK[j % 2]][:, :], ACT.Square).then_inc(sq_ready, 1)

            def take_MT(j):
                lane = (j % NT) * CT
                act.wait_ge(mt_done, j + 1)
                src = ps[M_BANK[j % 2]][:, :].rearrange("p (a c l) -> p a l c", a=IJ, l=L)
                dst = MT[:, j // NT, :, :, lane:lane + CT].rearrange("p l a c -> p a l c")
                nc.scalar.copy(dst, src).then_inc(mt_ready, 1)
                nc.scalar.copy(ST[:, j // NT, 0, :, :, lane:lane + CT].rearrange("p c i s -> p i c s"),
                               ps[M_BANK[j % 2]][:, :].rearrange("p (i c s l) -> p i c s l", i=2, c=2, l=L)[:, :, :, :, 0]
                               ).then_inc(mt_ready, 1)

            def gelus(j, blocks=range(HC)):
                for c in blocks:
                    act.wait_ge(f1_done, HC * j + c + 1)
                    nc.scalar.activation(g_sb[:, c, j], f_bank(j, c)[:, :], ACT.Gelu,
                                         bias=b1_sb[:, c:c + 1]).then_inc(gelu_ready, 1)

            def remap_h(b):
                wait_h(act, b)
                act.dma_start(hr[0:64, b, 1], h[64:128, b, 0]).then_inc(hr_moved[b], 16)
                nc.scalar.copy(hr[0:64, b, 0], h[0:64, b, 0]).then_inc(hr_copied, 1)
                nc.scalar.copy(hr[64:128, b, 1], h[64:128, b, 1]).then_inc(hr_copied, 1)

            def round_h(b):
                wait_hr(act, b)
                if b > 0:
                    act.wait_ge(y_done, NT * b)
                    act.wait_ge(hr_lo_ready, b)
                nc.scalar.copy(hr_hi[:, :, :], hr[:, b]).then_inc(hr_hi_ready, 1)

            act.dma_start(x_sb[:, 0, 2:4], x_v[0, 0][:, 2:4]).then_inc(x_loaded[0], 16)
            std_dev(0)
            act.wait_ge(w1_loaded, 16)
            nc.scalar.copy(w1_hi[:, :], w1_sb[:, :]).then_inc(w1hi_ready, 1)
            std_dev(1)
            take_xT(0)
            take_xT(1)
            std_dev(2)
            squares(0)
            squares(1)
            act.wait_ge(b1_loaded, 16)
            gelus(0)
            gelus(1, (0, 1))
            take_xT(2)
            take_xT(3)
            gelus(1, (2, 3))
            take_MT(0)
            gelus(2, (0,))
            take_MT(1)
            squares(2)
            gelus(2, (1,))
            squares(3)
            gelus(2, (2, 3))
            take_xT(4)
            gelus(3, (0,))
            take_xT(5)
            gelus(3, (1, 2))
            take_MT(2)
            gelus(3, (3,))
            take_MT(3)
            squares(4)
            squares(5)
            gelus(4, (0, 1))
            take_xT(6)
            take_xT(7)
            gelus(4, (2, 3))
            take_MT(4)
            gelus(5, (0,))
            take_MT(5)
            squares(6)
            gelus(5, (1,))
            squares(7)
            gelus(5, (2, 3))
            remap_h(0)
            act.wait_ge(bd_ready, G)
            nc.scalar.copy(wp_hi[:, :, :], wp_bd[:, :, :]).then_inc(wp_hi_ready, 1)
            round_h(0)
            gelus(6, (0, 1, 2))
            take_MT(6)
            take_MT(7)
            gelus(6, (3,))
            remap_h(1)
            gelus(7)
            round_h(1)
            remap_h(2)
            remap_h(3)

        @block.tensor
        def _(pe):
            def transpose_x(j):
                if j >= 2:
                    pe.wait_ge(xT_ready, j - 1)
                    pe.wait_ge(hi_ready, j - 1)
                for g in range(G):
                    wait_xn(pe, j, g)
                    mm = nc.tensor.transpose(ps[T_BANK[j % 2]][:, g * P:(g + 1) * P], xn[:, j, g, :], ident[:, :])
                mm.then_inc(xT_done, 1)

            def matrices(j):
                pe.wait_ge(xT_ready, j + 1)
                if j == 0:
                    pe.wait_ge(wm_loaded, 16)
                if j >= 2:
                    pe.wait_ge(mt_ready, 2 * (j - 1))
                for g in range(G):
                    mm = nc.tensor.matmul(ps[M_BANK[j % 2]][:, g * P:(g + 1) * P], xT[:, j % 4, g * P:(g + 1) * P],
                                          wmT[:, :], start=True, stop=True)
                mm.then_inc(m_done, 1)

            def transpose_M(j):
                pe.wait_ge(mn_ready, j + 1)
                for a in range(IJ):
                    mm = nc.tensor.transpose(ps[M_BANK[j % 2]][:, a * P:(a + 1) * P], Mn[:, j % 2, a], ident[:, :])
                mm.then_inc(mt_done, 1)

            def ffn_in(j, blocks=range(HC)):
                if j == 0:
                    pe.wait_ge(w1_ready, 1)
                pe.wait_ge(hi_ready, j + 1)
                for c in blocks:
                    if j == 1 and c < 2:
                        pe.wait_ge(gelu_ready, c + 1)
                    elif j > 0:
                        pe.wait_ge(gelu_ready, HC * j + c - 1)
                    bank, cols = f_bank(j, c), slice(c * P, (c + 1) * P)
                    nc.tensor.matmul(bank[:, :], w1_hi[:, cols], xT_hi[:, j % 4], start=True, stop=False)
                    nc.tensor.matmul(bank[:, :], w1_lo[:, cols], xT_hi[:, j % 4], start=False, stop=False)
                    if c == 0:
                        pe.wait_ge(lo_ready, j + 1)
                    nc.tensor.matmul(bank[:, :], w1_hi[:, cols], xT_lo[:, j % 4], start=False,
                                     stop=True).then_inc(f1_done, 1)

            def ffn_out(j, blocks=range(HC)):
                if j == 0:
                    pe.wait_ge(w2_loaded, 16)
                if j == NJ - 1 and 0 in blocks:
                    pe.wait_ge(gelu_ready, HC * NJ)
                if j in (2, 3) and 0 in blocks:
                    pe.wait_ge(xT_ready, j + 5)
                    pe.wait_ge(hi_ready, j + 5)
                if j in (4, 5) and 0 in blocks:
                    pe.wait_ge(mt_ready, 2 * (j + 3))
                if j == 6 and 0 in blocks:
                    pe.wait_ge(y_ready, 1)
                for c in blocks:
                    pe.wait_ge(gelu_ready, 3 if (j, c) == (0, 0) else HC * j + c + 1)
                    for g in range(G):
                        last = (j, c) == (NJ - 1, HC - 1)
                        first = c == 0 and (g == 0 or (g == 2 and j == NJ - 1))
                        mm = nc.tensor.matmul(o_bank(j, g // 2)[:, g * D:(g + 1) * D],
                                              g_sb[:, c, j, g * P:(g + 1) * P], w2_sb[:, c], start=first, stop=last,
                                              skip_group_check=True)
                        if last and g % 2 == 1:
                            mm.then_inc(y_done, 1)

            def project(j):
                b, tok = j // NT, slice((j % NT) * P, (j % NT + 1) * P)
                wait_hr(pe, b)
                if b < SPLIT_H:
                    if b == 0:
                        pe.wait_ge(wp_lo_ready, 1)
                    pe.wait_ge(wp_hi_ready, 1)
                    pe.wait_ge(hr_hi_ready, b + 1)
                    pe.wait_ge(hr_lo_ready, b + 1)
                    parts = ((hr_hi[:, :, tok], wp_hi), (hr_hi[:, :, tok], wp_lo), (hr_lo[:, :, tok], wp_hi))
                else:
                    parts = ((hr[:, b, :, tok], wp_bd),)
                for g2 in range(2):
                    for n, (h_part, w_part) in enumerate(parts):
                        mm = nc.tensor.matmul(o_bank(j, g2)[:, g2 * 2 * D:(g2 + 1) * 2 * D], h_part[:, g2],
                                              w_part[:, :, :], start=False,
                                              stop=(j < NJ - 1 and n == len(parts) - 1), skip_group_check=True)
                if j < NJ - 1:
                    mm.then_inc(y_done, 1)

            pe.wait_ge(ident_ready, 1)
            for _ in range(WARM_UP):
                nc.tensor.matmul(ps[F_BANK[0]][:, 0:P], ident[:, :], ident[:, :], start=True, stop=True)
            transpose_x(0)
            transpose_x(1)
            matrices(0)
            matrices(1)
            ffn_in(0, (0, 1, 2))
            transpose_x(2)
            ffn_in(0, (3,))
            transpose_x(3)
            ffn_in(1, (0, 1))
            ffn_out(0, (0, 1))
            ffn_in(1, (2, 3))
            ffn_out(0, (2, 3))
            transpose_M(0)
            ffn_in(2, (0,))
            transpose_M(1)
            matrices(2)
            ffn_in(2, (1,))
            matrices(3)
            ffn_out(1, (0, 1))
            ffn_in(2, (2, 3))
            transpose_x(4)
            ffn_out(1, (2,))
            ffn_in(3, (0,))
            transpose_x(5)
            ffn_out(1, (3,))
            ffn_in(3, (1, 2))
            transpose_M(2)
            ffn_in(3, (3,))
            transpose_M(3)
            matrices(4)
            transpose_x(6)
            matrices(5)
            ffn_in(4, (0, 1))
            transpose_x(7)
            ffn_in(4, (2, 3))
            ffn_out(2)
            transpose_M(4)
            ffn_in(5, (0,))
            transpose_M(5)
            matrices(6)
            ffn_in(5, (1,))
            matrices(7)
            ffn_out(3, (0,))
            ffn_in(5, (2, 3))
            ffn_out(3, (1, 2))
            ffn_in(6, (0, 1))
            ffn_out(3, (3,))
            ffn_in(6, (2,))
            transpose_M(6)
            transpose_M(7)
            project(0)
            project(1)
            ffn_out(4, (0, 1))
            ffn_in(6, (3,))
            ffn_out(4, (2, 3))
            ffn_in(7, (0, 1))
            ffn_out(5, (0, 1))
            ffn_in(7, (2, 3))
            ffn_out(5, (2, 3))
            ffn_out(6)
            project(2)
            project(3)
            ffn_out(7, (0, 1))
            project(4)
            project(5)
            ffn_out(7, (2,))
            project(6)
            project(7)
            ffn_out(7, (3,))

        @block.vector
        def _(dve):
            steps = {"seg": 0, "prod": 0, "state": 0, "rsqrt": 0}

            def counted(name, semaphore, ins):
                ins.then_inc(semaphore, 1)
                steps[name] += 1
                return steps[name]

            def nothing():
                pass

            def moments(run):
                chunks = range(LN_RUNS[run].start, LN_RUNS[run].stop)
                for j in chunks:
                    if j > 0:
                        dve.wait_ge(x_loaded[j], 16)
                    for g in range(G):
                        if j == 0 and g == 0:
                            dve.wait_ge(x0_loaded, 16)
                        if j == 0 and g == 2:
                            dve.wait_ge(x_loaded[0], 16)
                        nc.vector.bn_stats(stats[:, j, g], x_sb[:, j, g]).then_inc(bn_done, 1)
                        yield
                for j in chunks:
                    for g in range(G):
                        dve.wait_ge(bn_done, G * j + g + 1)
                        last = nc.vector.bn_aggr(mv[:, j, g], stats[:, j, g])
                        if (j, g) == (chunks[-1], G - 1):
                            last.then_inc(mv_ready, 1)
                        yield

            def layernorm_scale(run, between=nothing):
                js = LN_RUNS[run]
                dve.wait_ge(sd_ready, run + 1)
                nc.vector.reciprocal(rstd[:, js], sd[:, js]).then_inc(rstd_ready, 1)
                between()
                dve.wait_ge(rstd_ready, run + 1)
                nc.vector.scalar_tensor_tensor(nmr[:, js], mv[:, js, :, 0], -1.0, rstd[:, js],
                                               ALU.mult, ALU.mult).then_inc(nmr_ready, 1)

            def normalise_x(j, groups=range(G)):
                for g in groups:
                    nc.vector.tensor_scalar(xn[:, j, g], x_sb[:, j, g], rstd[:, j, g:g + 1], nmr[:, j, g:g + 1],
                                            ALU.mult, ALU.add).then_inc(xn_dve_ready, 1)

            def squared_norms(p, tick):
                s4 = sq[:, :, :, :, :].rearrange("p j g a k -> p (j g) a k")
                dve.wait_ge(sq_ready, 2 * p + 2)
                nc.vector.tensor_tensor(sq2[:, :, :, :], s4[:, :, 0:2], s4[:, :, 2:4], ALU.add).then_inc(nsq_step, 1)
                tick()
                dve.wait_ge(nsq_step, 2 * p + 1)
                nc.vector.tensor_tensor(nsq0[:, :, :], sq2[:, :, 0], sq2[:, :, 1], ALU.add).then_inc(nsq_step, 1)
                tick()
                dve.wait_ge(nsq_step, 2 * p + 2)
                dve.wait_ge(floor_ready, min(p, 2) + 1)
                fl = floor[:, 2 * p:2 * p + 2].rearrange("p j g -> p (j g)").unsqueeze(2).broadcast_to([P, 2 * G, K])
                nc.vector.tensor_tensor(nsq[:, :, :], nsq0[:, :, :], fl, ALU.max).then_inc(nsq_ready, 1)
                tick()

            def rsqrt(src, out, y0, y1, t0, t1, tick):
                n = counted("rsqrt", rsqrt_step, nc.vector.tensor_scalar(
                    y0.bitcast(mybir.dt.int32), src.bitcast(mybir.dt.int32), -0.5, RSQRT_MAGIC, ALU.mult, ALU.add))
                tick()
                for y, nxt, a, b in ((y0, y1, RSQRT_A, RSQRT_B), (y1, out, 0.5, RSQRT_C)):
                    dve.wait_ge(rsqrt_step, n)
                    n = counted("rsqrt", rsqrt_step,
                                nc.vector.scalar_tensor_tensor(t0, y, -a, y, ALU.mult, ALU.mult))
                    tick()
                    dve.wait_ge(rsqrt_step, n)
                    n = counted("rsqrt", rsqrt_step, nc.vector.tensor_tensor(t1, t0, src, ALU.mult))
                    tick()
                    dve.wait_ge(rsqrt_step, n)
                    last = nc.vector.scalar_tensor_tensor(nxt, t1, b, y, ALU.add, ALU.mult)
                    if nxt is y1:
                        n = counted("rsqrt", rsqrt_step, last)
                        tick()
                return last

            def inverse_norms(p, tick):
                dve.wait_ge(nsq_ready, p + 1)
                rsqrt(nsq[:, :, :], winv[:, :, :, :].rearrange("p j g k -> p (j g) k"), ry, ry1,
                      ra[:, :, :], rb[:, :, :], tick).then_inc(winv_ready, 1)
                tick()

            def late_scales(early_tick, tick):
                js, ticks = slice(4, NJ), itertools.chain([early_tick] * 4, itertools.repeat(tick))

                def next_tick():
                    next(ticks)()

                nc.vector.tensor_scalar(vv[:, :], mv[:, js, :, 1].rearrange("p j g -> p (j g)"), LN_EPS, None,
                                        ALU.add).then_inc(var_ready, 1)
                next_tick()
                dve.wait_ge(var_ready, 1)
                rsqrt(vv[:, :], rstd[:, js].rearrange("p j g -> p (j g)"), lv[:, 0], lv[:, 1], lv[:, 2], lv[:, 3],
                      next_tick).then_inc(rstd_ready, 1)
                next_tick()
                dve.wait_ge(rstd_ready, 4)
                nc.vector.scalar_tensor_tensor(nmr[:, js], mv[:, js, :, 0], -1.0, rstd[:, js],
                                               ALU.mult, ALU.mult).then_inc(nmr_ready, 1)
                next_tick()

            def normalise_M(p, tick):
                dve.wait_ge(winv_ready, p + 1)
                for j in (2 * p, 2 * p + 1):
                    if j >= 2:
                        dve.wait_ge(mt_done, j - 1)
                    src = ps[M_BANK[j % 2]][:, :].rearrange("p (g a k) -> p a g k", g=G, a=IJ)
                    w = winv[:, j % 2].unsqueeze(1).broadcast_to([P, IJ, G, K])
                    nc.vector.tensor_tensor(Mn[:, j % 2], src, w, ALU.mult).then_inc(mn_ready, 1)
                    tick()

            def compose(dst, tmp, later, earlier):
                n = dst.shape[-1]
                for k in range(2):
                    done = counted("seg", seg_step, nc.vector.tensor_tensor(
                        tmp[:, k, :, :, 0:n], later[:, k].unsqueeze(1).broadcast_to([P, 2, 2, n]),
                        earlier[:, :, k].unsqueeze(2).broadcast_to([P, 2, 2, n]), ALU.mult))
                    yield
                dve.wait_ge(seg_step, done)
                done = counted("seg", seg_step, nc.vector.tensor_tensor(dst, tmp[:, 0, :, :, 0:n],
                                                                        tmp[:, 1, :, :, 0:n], ALU.add))
                yield
                dve.wait_ge(seg_step, done)

            def carry(dst, tmp, mat, vec, final=None):
                n = dst.shape[-1]
                done = counted("seg", seg_step, nc.vector.tensor_tensor(
                    tmp[:, :, :, 0:n], mat, vec.unsqueeze(2).broadcast_to([P, 2, 2, n]), ALU.mult))
                yield
                dve.wait_ge(seg_step, done)
                last = nc.vector.tensor_tensor(dst, tmp[:, 0, :, 0:n], tmp[:, 1, :, 0:n], ALU.add)
                if final is None:
                    done = counted("seg", seg_step, last)
                    yield
                    dve.wait_ge(seg_step, done)
                else:
                    last.then_inc(start_ready, 1)
                    yield
                    dve.wait_ge(start_ready, final)

            def scan(b):
                dve.wait_ge(mt_ready, 2 * NT * (b + 1))
                for l in range(1, L):
                    pr = PR[:, b % 2]
                    m = MT[:, b, l].rearrange("p (i k) s -> p i (k s)", i=2)
                    st = ST[:, b, l - 1].rearrange("p c k s -> p c (k s)")
                    if l > 1:
                        dve.wait_ge(state_ready, state)
                    prod = counted("prod", prod_ready, nc.vector.tensor_tensor(
                        pr.rearrange("p i c k s -> p i c (k s)"), m.unsqueeze(2).broadcast_to([P, 2, 2, 2 * S]),
                        st.unsqueeze(1).broadcast_to([P, 2, 2, 2 * S]), ALU.mult))
                    yield
                    dve.wait_ge(prod_ready, prod)
                    state = counted("state", state_ready, nc.vector.tensor_tensor(
                        ST[:, b, l].rearrange("p c i s -> p i c s"), pr[:, :, :, 0], pr[:, :, :, 1], ALU.add))
                    yield
                tot, hs = ST[:, b, L - 1], HS[:, b]
                s2, s4, s8, cp, hp = SEG2[:, b % 2], SEG4[:, b % 2], SEG8[:, b % 2], CP[:, b % 2], HP[:, b % 2]
                dve.wait_ge(state_ready, state)
                yield from compose(s2, cp, tot[:, :, :, 1::2], tot[:, :, :, 0::2])
                yield from compose(s4, cp, s2[:, :, :, 1::2], s2[:, :, :, 0::2])
                yield from compose(s8, cp, s4[:, :, :, 1::2], s4[:, :, :, 0::2])
                if b == 0:
                    dve.wait_ge(hs_ready, 1)
                for q in range(S // 8 - 1):
                    yield from carry(hs[:, :, 8 * q + 8:8 * q + 9], hp, s8[:, :, :, q:q + 1],
                                     hs[:, :, 8 * q:8 * q + 1])
                yield from carry(hs[:, :, 4::8], hp, s4[:, :, :, 0::2], hs[:, :, 0::8])
                yield from carry(hs[:, :, 2::4], hp, s2[:, :, :, 0::2], hs[:, :, 0::4])
                yield from carry(hs[:, :, 1::2], hp, tot[:, :, :, 0::2], hs[:, :, 0::2], b + 1)
                if b == POOL_H:
                    nc.vector.tensor_tensor(
                        lp_of(b)[:, 0], ST[:, b, :, 0],
                        hs[:, 0].unsqueeze(1).unsqueeze(1).broadcast_to([P, L, 2, S]), ALU.mult).then_inc(half_ready, 1)
                    yield
                if b <= POOL_H:
                    return
                lp = lp_of(b)
                for c in range(2):
                    done = counted("seg", seg_step, nc.vector.tensor_tensor(
                        lp[:, c], ST[:, b, :, c],
                        hs[:, c].unsqueeze(1).unsqueeze(1).broadcast_to([P, L, 2, S]), ALU.mult))
                    yield
                dve.wait_ge(seg_step, done)
                nc.vector.tensor_tensor(h[:, b].rearrange("p i (c l) -> p l i c", l=L), lp[:, 0], lp[:, 1],
                                        ALU.add).then_inc(last_h_ready, 1)
                yield

            def add_halves(b):
                dve.wait_ge(half_ready, 1)
                dve.wait_ge(lp_ready, 2 * POOL_H + 1)
                lp = lp_of(b)
                nc.vector.tensor_tensor(h[:, b].rearrange("p i (c l) -> p l i c", l=L), lp[:, 0], lp[:, 1],
                                        ALU.add).then_inc(last_h_ready, 1)

            def last_output():
                for half in range(2):
                    gs, cols = slice(2 * half, 2 * half + 2), slice(2 * half * D, 2 * (half + 1) * D)
                    dve.wait_ge(y_done, NJ + half)
                    dve.wait_ge(resid_ready, NJ)
                    nc.vector.tensor_tensor(x_sb[:, NJ - 1, gs].rearrange("p g d -> p (g d)"),
                                            o_bank(NJ - 1, half)[:, cols],
                                            x_sb[:, NJ - 1, gs].rearrange("p g d -> p (g d)"),
                                            ALU.add).then_inc(y_ready, 1)

            def output(j):
                dve.wait_ge(y_done, j + 1)
                dve.wait_ge(resid_ready, j + 1)
                nc.vector.tensor_tensor(x_sb[:, j].rearrange("p g d -> p (g d)"), ps[O_BANK[j]][:, :],
                                        x_sb[:, j].rearrange("p g d -> p (g d)"), ALU.add).then_inc(y_ready, 1)

            def run_all(steps):
                for _ in steps:
                    pass

            moments_1 = moments(1)
            run_all(moments(0))
            run_all(itertools.islice(moments_1, G // 2))
            layernorm_scale(0, lambda: run_all(itertools.islice(moments_1, G // 2)))
            run_all(moments_1)
            dve.wait_ge(nmr_ready, 1)
            normalise_x(0, (0, 1))
            layernorm_scale(1, lambda: normalise_x(0, (2, 3)))
            dve.wait_ge(nmr_ready, 2)
            normalise_x(1)
            run_all(moments(2))
            layernorm_scale(2)
            dve.wait_ge(nmr_ready, 3)
            normalise_x(2)
            late = moments(3)

            def tick():
                next(late, None)
                next(late, None)

            squared_norms(0, tick)
            inverse_norms(0, tick)
            normalise_M(0, nothing)
            run_all(late)
            dve.wait_ge(mv_ready, 4)
            dve.wait_ge(v_loaded, 16 * G)
            nc.vector.tensor_copy(HS[:, :, :, 0], v_sb[:, :].unsqueeze(1).broadcast_to([P, NB, 2])).then_inc(hs_ready, 1)
            scans = [scan(b) for b in range(NB)]

            def take(b, n):
                went_on = True
                for _ in range(n):
                    went_on = next(scans[b], "ended") is None
                return went_on

            def alternate(active, n):
                for _ in range(n):
                    for b in active:
                        take(b, 1)

            def to_matrices(p):
                def tick():
                    if p == 1 or not take(p - 2, 1):
                        take(p - 1, 1)

                squared_norms(p, tick)
                inverse_norms(p, tick)
                normalise_M(p, tick)

            late_scales(nothing, lambda: take(0, 1))
            to_matrices(1)
            take(0, 6)
            alternate((0, 1), 4)
            to_matrices(2)
            run_all(scans[0])
            take(1, 6)
            alternate((1, 2), 4)
            to_matrices(3)
            run_all(scans[1])
            take(2, 2)
            alternate((2, 3), 7)
            output(0)
            alternate((2, 3), 20)
            run_all(scans[2])
            take(3, 8)
            add_halves(2)
            run_all(scans[3])
            for j in range(1, NJ - 1):
                output(j)
            last_output()


_INS = ['L0_attn_x', 'L0_attn_W_m', 'L0_attn_v_vec', 'L0_attn_W_proj', 'L0_attn_out_scale',
        'L0_ffn_w1', 'L0_ffn_b1', 'L0_ffn_w2', 'L0_ffn_b2']
_OUTS = [((16, 256, 128), 'float32')]


def kernel(**inputs):
    import numpy as _np
    import concourse.bacc as _bacc
    from concourse import mybir as _mybir
    from concourse.bass_utils import run_bass_kernel_spmd as _run

    nc = _bacc.Bacc("TRN2", target_bir_lowering=False, num_devices=1)
    laid = dict(inputs)
    laid['L0_attn_W_m'] = _np.asarray(inputs['L0_attn_W_m']).reshape(32, 4, 128).transpose(2, 1, 0).reshape(128, 128)
    laid['L0_attn_W_proj'] = _np.asarray(inputs['L0_attn_W_proj']).reshape(128, 32, 2).transpose(1, 2, 0)
    laid['L0_ffn_b1'] = _np.asarray(inputs['L0_ffn_b1']).reshape(4, 128).T
    arrays, args = {}, []
    for name in _INS:
        a = _np.ascontiguousarray(laid[name])
        arrays[f"in_{name}_dram"] = a
        args.append(nc.dram_tensor(f"in_{name}_dram", a.shape, _mybir.dt.from_np(a.dtype), kind="ExternalInput").ap())
    for i, (shape, dtype) in enumerate(_OUTS):
        dt = _mybir.dt.from_np(_np.dtype(dtype))
        args.append(nc.dram_tensor(f"out_{i}_dram", shape, dt, kind="ExternalOutput").ap())
    block_kernel(nc, *args)
    r = _run(nc, [arrays], core_ids=[0])
    got = tuple(r.results[0][f"out_{i}_dram"] for i in range(len(_OUTS)))
    return got[0]
```
